# Optimizing a Trainium2 kernel written in Bass

```python
import numpy as np
import jax
import jax.numpy as jnp

def _softmax(x, axis=-1):
    return jax.nn.softmax(x, axis=axis)

def _gelu(x):
    return jax.nn.gelu(x, approximate=True)

def _silu(x):
    return jax.nn.silu(x)

def _sigmoid(x):
    return jax.nn.sigmoid(x)

def _layernorm(x, axis=-1, eps=1e-05):
    m = jnp.mean(x, axis=axis, keepdims=True)
    v = jnp.var(x, axis=axis, keepdims=True)
    return (x - m) / jnp.sqrt(v + eps)

def _scatter_add(tgt, idx, src, axis=0):
    return tgt.at[idx].add(src)

def _segment_sum(src, seg, n):
    return jax.ops.segment_sum(src, seg, n)
kernel_name = 'mk_dlrm_tower_d1_rec_r8_05747a'

def setup_inputs(seed: int=0):
    np.random.seed(seed)
    _w = jnp.asarray

    def _rec_inputs():
        import jax
        import jax.numpy as jnp
        _tk = jax.random.key(seed)
        dense_ctx = jax.random.normal(jax.random.fold_in(_tk, 190), (512, 16), jnp.float32)
        ids = jnp.stack([jax.random.randint(jax.random.fold_in(_tk, 200 + f), (512,), 0, v, jnp.int32) for f, v in enumerate([12500, 125000, 1250, 1250, 125000, 125000, 1000, 125000, 1000, 1000, 1000, 1250, 1250, 125000, 1000, 12500, 1000, 1000, 125000, 1250, 125000, 1250, 1250, 12500, 1000, 12500, 12500, 1000, 125000, 1000, 1250, 12500, 1250, 125000, 125000, 1000, 1250, 125000, 12500])], axis=1)
        tbl_0 = 0.05 * jax.random.normal(jax.random.fold_in(_tk, 500 + 0), (12500, 16), jnp.float32)
        tbl_1 = 0.05 * jax.random.normal(jax.random.fold_in(_tk, 500 + 1), (125000, 16), jnp.float32)
        tbl_2 = 0.05 * jax.random.normal(jax.random.fold_in(_tk, 500 + 2), (1250, 16), jnp.float32)
        tbl_3 = 0.05 * jax.random.normal(jax.random.fold_in(_tk, 500 + 3), (1250, 16), jnp.float32)
        tbl_4 = 0.05 * jax.random.normal(jax.random.fold_in(_tk, 500 + 4), (125000, 16), jnp.float32)
        tbl_5 = 0.05 * jax.random.normal(jax.random.fold_in(_tk, 500 + 5), (125000, 16), jnp.float32)
        tbl_6 = 0.05 * jax.random.normal(jax.random.fold_in(_tk, 500 + 6), (1000, 16), jnp.float32)
        tbl_7 = 0.05 * jax.random.normal(jax.random.fold_in(_tk, 500 + 7), (125000, 16), jnp.float32)
        tbl_8 = 0.05 * jax.random.normal(jax.random.fold_in(_tk, 500 + 8), (1000, 16), jnp.float32)
        tbl_9 = 0.05 * jax.random.normal(jax.random.fold_in(_tk, 500 + 9), (1000, 16), jnp.float32)
        tbl_10 = 0.05 * jax.random.normal(jax.random.fold_in(_tk, 500 + 10), (1000, 16), jnp.float32)
        tbl_11 = 0.05 * jax.random.normal(jax.random.fold_in(_tk, 500 + 11), (1250, 16), jnp.float32)
        tbl_12 = 0.05 * jax.random.normal(jax.random.fold_in(_tk, 500 + 12), (1250, 16), jnp.float32)
        tbl_13 = 0.05 * jax.random.normal(jax.random.fold_in(_tk, 500 + 13), (125000, 16), jnp.float32)
        tbl_14 = 0.05 * jax.random.normal(jax.random.fold_in(_tk, 500 + 14), (1000, 16), jnp.float32)
        tbl_15 = 0.05 * jax.random.normal(jax.random.fold_in(_tk, 500 + 15), (12500, 16), jnp.float32)
        tbl_16 = 0.05 * jax.random.normal(jax.random.fold_in(_tk, 500 + 16), (1000, 16), jnp.float32)
        tbl_17 = 0.05 * jax.random.normal(jax.random.fold_in(_tk, 500 + 17), (1000, 16), jnp.float32)
        tbl_18 = 0.05 * jax.random.normal(jax.random.fold_in(_tk, 500 + 18), (125000, 16), jnp.float32)
        tbl_19 = 0.05 * jax.random.normal(jax.random.fold_in(_tk, 500 + 19), (1250, 16), jnp.float32)
        tbl_20 = 0.05 * jax.random.normal(jax.random.fold_in(_tk, 500 + 20), (125000, 16), jnp.float32)
        tbl_21 = 0.05 * jax.random.normal(jax.random.fold_in(_tk, 500 + 21), (1250, 16), jnp.float32)
        tbl_22 = 0.05 * jax.random.normal(jax.random.fold_in(_tk, 500 + 22), (1250, 16), jnp.float32)
        tbl_23 = 0.05 * jax.random.normal(jax.random.fold_in(_tk, 500 + 23), (12500, 16), jnp.float32)
        tbl_24 = 0.05 * jax.random.normal(jax.random.fold_in(_tk, 500 + 24), (1000, 16), jnp.float32)
        tbl_25 = 0.05 * jax.random.normal(jax.random.fold_in(_tk, 500 + 25), (12500, 16), jnp.float32)
        tbl_26 = 0.05 * jax.random.normal(jax.random.fold_in(_tk, 500 + 26), (12500, 16), jnp.float32)
        tbl_27 = 0.05 * jax.random.normal(jax.random.fold_in(_tk, 500 + 27), (1000, 16), jnp.float32)
        tbl_28 = 0.05 * jax.random.normal(jax.random.fold_in(_tk, 500 + 28), (125000, 16), jnp.float32)
        tbl_29 = 0.05 * jax.random.normal(jax.random.fold_in(_tk, 500 + 29), (1000, 16), jnp.float32)
        tbl_30 = 0.05 * jax.random.normal(jax.random.fold_in(_tk, 500 + 30), (1250, 16), jnp.float32)
        tbl_31 = 0.05 * jax.random.normal(jax.random.fold_in(_tk, 500 + 31), (12500, 16), jnp.float32)
        tbl_32 = 0.05 * jax.random.normal(jax.random.fold_in(_tk, 500 + 32), (1250, 16), jnp.float32)
        tbl_33 = 0.05 * jax.random.normal(jax.random.fold_in(_tk, 500 + 33), (125000, 16), jnp.float32)
        tbl_34 = 0.05 * jax.random.normal(jax.random.fold_in(_tk, 500 + 34), (125000, 16), jnp.float32)
        tbl_35 = 0.05 * jax.random.normal(jax.random.fold_in(_tk, 500 + 35), (1000, 16), jnp.float32)
        tbl_36 = 0.05 * jax.random.normal(jax.random.fold_in(_tk, 500 + 36), (1250, 16), jnp.float32)
        tbl_37 = 0.05 * jax.random.normal(jax.random.fold_in(_tk, 500 + 37), (125000, 16), jnp.float32)
        tbl_38 = 0.05 * jax.random.normal(jax.random.fold_in(_tk, 500 + 38), (12500, 16), jnp.float32)
        _rk = jax.random.fold_in(_tk, 7)
        W_top1 = 0.05 * jax.random.normal(jax.random.fold_in(_tk, 801), (400, 512), jnp.float32)
        W_top2 = 0.0441942 * jax.random.normal(jax.random.fold_in(_tk, 802), (512, 256), jnp.float32)
        W_top3 = 0.0625 * jax.random.normal(jax.random.fold_in(_tk, 803), (256, 1), jnp.float32)
        b_top1 = jnp.zeros((512,), jnp.float32)
        b_top2 = jnp.zeros((256,), jnp.float32)
        return (dense_ctx, ids, tbl_0, tbl_1, tbl_2, tbl_3, tbl_4, tbl_5, tbl_6, tbl_7, tbl_8, tbl_9, tbl_10, tbl_11, tbl_12, tbl_13, tbl_14, tbl_15, tbl_16, tbl_17, tbl_18, tbl_19, tbl_20, tbl_21, tbl_22, tbl_23, tbl_24, tbl_25, tbl_26, tbl_27, tbl_28, tbl_29, tbl_30, tbl_31, tbl_32, tbl_33, tbl_34, tbl_35, tbl_36, tbl_37, tbl_38, W_top1, b_top1, W_top2, b_top2, W_top3)
    dense_ctx, ids, tbl_0, tbl_1, tbl_2, tbl_3, tbl_4, tbl_5, tbl_6, tbl_7, tbl_8, tbl_9, tbl_10, tbl_11, tbl_12, tbl_13, tbl_14, tbl_15, tbl_16, tbl_17, tbl_18, tbl_19, tbl_20, tbl_21, tbl_22, tbl_23, tbl_24, tbl_25, tbl_26, tbl_27, tbl_28, tbl_29, tbl_30, tbl_31, tbl_32, tbl_33, tbl_34, tbl_35, tbl_36, tbl_37, tbl_38, W_top1, b_top1, W_top2, b_top2, W_top3 = _rec_inputs()

    def _L0_rec_setup():
        import jax, jax.numpy as jnp
        import numpy as np
        B, F0, D = (256, 39, 16)
        CROSS = [128, 128, 128]
        key = jax.random.key(seed)
        k0, k1, k2, k3 = jax.random.split(key, 4)
        inputs = jax.random.normal(k0, (B, F0, D), dtype=jnp.float32)
        f0 = jax.random.normal(k1, (F0 * F0, CROSS[0]), dtype=jnp.float32) * 0.05
        f1 = jax.random.normal(k2, (CROSS[0] * F0, CROSS[1]), dtype=jnp.float32) * 0.05
        f2 = jax.random.normal(k3, (CROSS[1] * F0, CROSS[2]), dtype=jnp.float32) * 0.05
        return {'inputs': inputs, 'f0': f0, 'f1': f1, 'f2': f2}
    _L0_rec_all = _L0_rec_setup()
    _L0_rec_in = {k: v for k, v in _L0_rec_all.items() if k in ('f0', 'f1', 'f2')}
    del _L0_rec_all
    return {'dense_ctx': dense_ctx, 'ids': ids, 'tbl_0': tbl_0, 'tbl_1': tbl_1, 'tbl_2': tbl_2, 'tbl_3': tbl_3, 'tbl_4': tbl_4, 'tbl_5': tbl_5, 'tbl_6': tbl_6, 'tbl_7': tbl_7, 'tbl_8': tbl_8, 'tbl_9': tbl_9, 'tbl_10': tbl_10, 'tbl_11': tbl_11, 'tbl_12': tbl_12, 'tbl_13': tbl_13, 'tbl_14': tbl_14, 'tbl_15': tbl_15, 'tbl_16': tbl_16, 'tbl_17': tbl_17, 'tbl_18': tbl_18, 'tbl_19': tbl_19, 'tbl_20': tbl_20, 'tbl_21': tbl_21, 'tbl_22': tbl_22, 'tbl_23': tbl_23, 'tbl_24': tbl_24, 'tbl_25': tbl_25, 'tbl_26': tbl_26, 'tbl_27': tbl_27, 'tbl_28': tbl_28, 'tbl_29': tbl_29, 'tbl_30': tbl_30, 'tbl_31': tbl_31, 'tbl_32': tbl_32, 'tbl_33': tbl_33, 'tbl_34': tbl_34, 'tbl_35': tbl_35, 'tbl_36': tbl_36, 'tbl_37': tbl_37, 'tbl_38': tbl_38, 'W_top1': W_top1, 'b_top1': b_top1, 'W_top2': W_top2, 'b_top2': b_top2, 'W_top3': W_top3, 'L0_rec_f0': _L0_rec_in['f0'], 'L0_rec_f1': _L0_rec_in['f1'], 'L0_rec_f2': _L0_rec_in['f2']}

def reference(dense_ctx, ids, tbl_0, tbl_1, tbl_2, tbl_3, tbl_4, tbl_5, tbl_6, tbl_7, tbl_8, tbl_9, tbl_10, tbl_11, tbl_12, tbl_13, tbl_14, tbl_15, tbl_16, tbl_17, tbl_18, tbl_19, tbl_20, tbl_21, tbl_22, tbl_23, tbl_24, tbl_25, tbl_26, tbl_27, tbl_28, tbl_29, tbl_30, tbl_31, tbl_32, tbl_33, tbl_34, tbl_35, tbl_36, tbl_37, tbl_38, W_top1, b_top1, W_top2, b_top2, W_top3, L0_rec_f0, L0_rec_f1, L0_rec_f2):
    import jax
    import jax.numpy as jnp

    def _L0_rec_ref(inputs, f0, f1, f2):
        import jax, jax.numpy as jnp
        import numpy as np
        B, F0, D = (256, 39, 16)
        CROSS = [128, 128, 128]
        filters = [f0, f1, f2]
        x0 = inputs
        xk = inputs
        outs = []
        for W in filters:
            b, f, d = x0.shape
            g = xk.shape[1]
            z = jnp.einsum('bfd,bgd->bfgd', x0, xk).reshape(b, f * g, d)
            cur = jnp.einsum('bpd,pm->bmd', z, W)
            outs.append(cur)
            xk = cur
        result = jnp.concatenate(outs, axis=1)
        return jnp.sum(result, axis=-1)
    e = jnp.stack([tbl_0[ids[:, 0]], tbl_1[ids[:, 1]], tbl_2[ids[:, 2]], tbl_3[ids[:, 3]], tbl_4[ids[:, 4]], tbl_5[ids[:, 5]], tbl_6[ids[:, 6]], tbl_7[ids[:, 7]], tbl_8[ids[:, 8]], tbl_9[ids[:, 9]], tbl_10[ids[:, 10]], tbl_11[ids[:, 11]], tbl_12[ids[:, 12]], tbl_13[ids[:, 13]], tbl_14[ids[:, 14]], tbl_15[ids[:, 15]], tbl_16[ids[:, 16]], tbl_17[ids[:, 17]], tbl_18[ids[:, 18]], tbl_19[ids[:, 19]], tbl_20[ids[:, 20]], tbl_21[ids[:, 21]], tbl_22[ids[:, 22]], tbl_23[ids[:, 23]], tbl_24[ids[:, 24]], tbl_25[ids[:, 25]], tbl_26[ids[:, 26]], tbl_27[ids[:, 27]], tbl_28[ids[:, 28]], tbl_29[ids[:, 29]], tbl_30[ids[:, 30]], tbl_31[ids[:, 31]], tbl_32[ids[:, 32]], tbl_33[ids[:, 33]], tbl_34[ids[:, 34]], tbl_35[ids[:, 35]], tbl_36[ids[:, 36]], tbl_37[ids[:, 37]], tbl_38[ids[:, 38]]], axis=1)
    z = _L0_rec_ref(e, L0_rec_f0, L0_rec_f1, L0_rec_f2)
    z = z.reshape(z.shape[0], -1)
    h = jnp.concatenate([z, dense_ctx], axis=1)
    h = jnp.maximum(h @ W_top1 + b_top1, 0.0)
    h = jnp.maximum(h @ W_top2 + b_top2, 0.0)
    y = h @ W_top3
    return y

_drawn_inputs = setup_inputs


def setup_inputs(seed=0):
    import zlib

    import numpy as np

    out = dict(_drawn_inputs(seed))
    spreads = {'b_top1': (0.0, 0.609), 'b_top2': (0.0, 0.268)}
    factors = {'tbl_0': 4.57,
     'tbl_1': 4.969,
     'tbl_2': 4.983,
     'tbl_3': 5.031,
     'tbl_4': 4.971,
     'tbl_5': 5.012,
     'tbl_6': 5.03,
     'tbl_7': 4.818,
     'tbl_8': 4.956,
     'tbl_9': 4.725,
     'tbl_10': 5.363,
     'tbl_11': 4.516,
     'tbl_12': 4.414,
     'tbl_13': 4.592,
     'tbl_14': 4.873,
     'tbl_15': 4.828,
     'tbl_16': 5.091,
     'tbl_17': 5.001,
     'tbl_18': 5.185,
     'tbl_19': 5.121,
     'tbl_20': 4.887,
     'tbl_21': 4.669,
     'tbl_22': 4.501,
     'tbl_23': 4.803,
     'tbl_24': 4.401,
     'tbl_25': 4.493,
     'tbl_26': 4.865,
     'tbl_27': 5.154,
     'tbl_28': 4.559,
     'tbl_29': 5.048,
     'tbl_30': 4.988,
     'tbl_31': 4.469,
     'tbl_32': 5.108,
     'tbl_33': 4.77,
     'tbl_34': 4.746,
     'tbl_35': 4.502,
     'tbl_36': 4.918,
     'tbl_37': 5.006,
     'tbl_38': 4.955,
     'L0_rec_f1': 5.202,
     'L0_rec_f2': 8.0}
    for name, (base, spread) in spreads.items():
        noise = np.random.default_rng([zlib.crc32(name.encode()), seed]).standard_normal(out[name].shape)
        drawn = base * np.exp(spread * noise) if base else spread * noise
        out[name] = jnp.asarray(drawn.astype(out[name].dtype))
    for name, factor in factors.items():
        out[name] = (out[name] * factor).astype(out[name].dtype)
    return out
```

```python
from contextlib import ExitStack

import numpy as np
import concourse.bass as bass
from concourse import mybir

F32 = mybir.dt.float32
F32R = mybir.dt.float32r
I32 = mybir.dt.int32
ALU = mybir.AluOpType
ACT = mybir.ActivationFunctionType

P = 128
B, F, D, M = 512, 39, 16, 128
CHUNKS = B // P
TPG = 4
GROUPS = D // TPG
COLS = TPG * P
NK = F // 2 + 1
FX = F + NK - 1
KPT = P // F
KT = -(-NK // KPT)
ROWS = [F * min(KPT, NK - KPT * t) for t in range(KT)]
FPB = 4
BLOCKS = -(-F // FPB)
NF = [min(FPB, F - FPB * j) for j in range(BLOCKS)]
PAIRS = TPG // 2
UNITS = TPG * BLOCKS
FMAS = TPG * FPB * BLOCKS // 2
SCALED = TPG * BLOCKS // 2
ADDS = PAIRS * 2 * (BLOCKS // 2 + 1)
SLOTS = BLOCKS
SB8 = P // D
QS = P // SB8
FG = F + 1
H1, H2 = 512, 256
ZT = 3
DENSE = 16


def pair_rows():
    k = np.arange(NK)[:, None]
    f = np.arange(F)[None, :]
    g = (f + k) % F
    return (f * F + g).reshape(-1), (g * F + f).reshape(-1)


def build(nc, ids, tables, w0a_d, w0b_d, f1, f2, wt1_d, bt1_d, wt2_d, bt2_d, wt3_d, dense_t, out):
    ctx = ExitStack()
    with ctx:
        def sb(name, shape, dt=F32):
            return ctx.enter_context(nc.sbuf_tensor(name, shape, dt))

        def sem(name):
            return ctx.enter_context(nc.semaphore(name))

        w1h = sb("w1h", [P, F * M], F32R)
        w1l = sb("w1l", [P, F * M], F32R)
        w0h = sb("w0h", [P, KT * M], F32R)
        w0l = sb("w0l", [P, KT * M], F32R)
        w2 = sb("w2", [P, F, M])
        wt1 = sb("wt1", [P, ZT, H1])
        wtd = sb("wtd", [DENSE + 1, H1])
        wt2 = sb("wt2", [P, H1 // P, H2])
        bt2 = sb("bt2", [1, H2])
        wt3 = sb("wt3", [P, H2 // P])
        ident = sb("ident", [P, P])
        ones_row = sb("ones_row", [1, P])
        idx_all = sb("idx_all", [P, CHUNKS, F], I32)
        idx_cur = sb("idx_cur", [P, F], I32)
        e_next = sb("e_next", [P, FX, D])
        e_dve = sb("e_dve", [P, FX, D])
        e_act = sb("e_act", [P, F, D])
        ep = sb("ep", [P, D, FG])
        pairs = sb("pairs", [P, 2, TPG, KPT * F])
        ph = sb("ph", [P, 2, COLS], F32R)
        pl = sb("pl", [P, 2, COLS], F32R)
        x1h = sb("x1h", [P, 2, COLS], F32R)
        x1l = sb("x1l", [P, 2, COLS], F32R)
        scaled = sb("scaled", [P, BLOCKS, FPB * M])
        lanes = sb("lanes", [P, 2, FPB * M])
        xd = sb("xd", [P, 2, TPG, M])
        xp = sb("xp", [P, 2, TPG, M])
        z1acc = sb("z1acc", [P, COLS])
        z1half = sb("z1half", [P, COLS // 2])
        z1t = sb("z1t", [P, P])
        x2q = sb("x2q", [P, QS, M])
        eblk = sb("eblk", [P, QS, SB8 * FG])
        gs = sb("gs", [P, FG, P])
        z3t = sb("z3t", [P, P])
        dense_sb = sb("dense_sb", [DENSE + 1, B])
        h1s = sb("h1s", [P, H1])
        h2s = sb("h2s", [P, H2])
        y_sb = sb("y_sb", [1, B])

        w1_raw = gs[:].rearrange("p f b -> p (f b)")[:, 0:F * M]
        raw = scaled[:].rearrange("p s n -> p (s n)")
        w0_a, w0_b, w0_s = (raw[0:ROWS[0], n * KT * M:(n + 1) * KT * M] for n in range(3))

        l2_ps = ctx.enter_context(nc.psum_tensor("l2_ps", [P, 4, 512], F32))
        t_ps = ctx.enter_context(nc.psum_tensor("t_ps", [P, 2, 512], F32))
        l1_ps = ctx.enter_context(nc.psum_tensor("l1_ps", [P, 512], F32))
        l3_ps = ctx.enter_context(nc.psum_tensor("l3_ps", [P, 512], F32))

        x2_dram = nc.dram_tensor("x2_dram", [P, D, M], F32, kind="Internal").ap()
        e_dram = nc.dram_tensor("e_dram", [P, D, FG], F32, kind="Internal").ap()

        ids_in, w0_in, w1_in, w2_in, top_in = (sem(n) for n in ("ids_in", "w0_in", "w1_in", "w2_in", "top_in"))
        w0_sum, w0h_ok, w0l_ok, w1h_ok, w1l_ok = (sem(n) for n in ("w0_sum", "w0h_ok", "w0l_ok", "w1h_ok", "w1l_ok"))
        ident_zero, ident_ok, filled = sem("ident_zero"), sem("ident_ok"), sem("filled")
        idx_ok, gathered, e_wrapped = sem("idx_ok"), sem("gathered"), sem("e_wrapped")
        e_dve_ok, e_act_ok = sem("e_dve_ok"), sem("e_act_ok")
        pairs_ok = sem("pairs_ok")
        turned = sem("turned")
        pair_hi = sem("pair_hi")
        pair_lo = sem("pair_lo")
        l1_done = sem("l1_done")
        x1_hi, x1_lo, z1_added = sem("x1_hi"), sem("x1_lo"), sem("z1_added")
        y_ready = sem("y_ready")
        fma_done = sem("fma_done")
        act_scaled = sem("act_scaled")
        pool_added = sem("pool_added")
        x2_ready, x2_stored, x2q_in = sem("x2_ready"), sem("x2_stored"), sem("x2q_in")
        ep_ready, ep_stored, eblk_in = sem("ep_ready"), sem("ep_stored"), sem("eblk_in")
        g_done, g_kept, z3_done, z3_ready = sem("g_done"), sem("g_kept"), sem("z3_done"), sem("z3_ready")
        z1_fold, dense_in = sem("z1_fold"), sem("dense_in")
        h1_done, h1_ready, h2_done, h2_ready = sem("h1_done"), sem("h1_ready"), sem("h2_done"), sem("h2_ready")
        y_done, y_kept, y_out = sem("y_done"), sem("y_kept"), sem("y_out")

        block = ctx.enter_context(nc.Block())

        @block.sync
        def _(sp):
            sp.dma_start(idx_all[:], ids.rearrange("(c p) f -> p c f", p=P)).then_inc(ids_in, 16)
            sp.dma_start(w0_a, w0a_d).then_inc(w0_in, 16)
            sp.dma_start(w0_b, w0b_d).then_inc(w0_in, 16)
            sp.dma_start(w1_raw.rearrange("p (f m) -> p f m", m=M),
                         f1.rearrange("(f g) m -> g f m", g=M)).then_inc(w1_in, 16)
            sp.dma_start(w2[:], f2.rearrange("(f g) m -> g f m", g=M)).then_inc(w2_in, 16)
            sp.dma_start(wt1[:], wt1_d[0:ZT * P, :].rearrange("(k p) n -> p k n", p=P)).then_inc(top_in, 16)
            sp.dma_start(wtd[0:DENSE, :], wt1_d[ZT * P:ZT * P + DENSE, :]).then_inc(top_in, 16)
            sp.dma_start(wtd[DENSE:DENSE + 1, :], bt1_d).then_inc(top_in, 16)
            sp.dma_start(wt2[:], wt2_d.rearrange("(k p) n -> p k n", p=P)).then_inc(top_in, 16)
            sp.dma_start(bt2[:], bt2_d).then_inc(top_in, 16)
            sp.dma_start(wt3[:], wt3_d).then_inc(top_in, 16)
            sp.wait_ge(filled, 4)
            sp.dma_start(dense_sb[0:DENSE, :], dense_t).then_inc(dense_in, 16)

            def store_x2(c, gi):
                sp.wait_ge(x2_ready, 4 * c + gi + 1)
                sp.dma_start(x2_dram[:, TPG * gi:TPG * gi + TPG, :],
                             xd[:, gi % 2]).then_inc(x2_stored, 16)

            def load_x2q(c):
                sp.wait_ge(x2_stored, 64 * (c + 1))
                for s in range(SB8):
                    sp.dma_start(x2q[s * D:(s + 1) * D, :, :],
                                 x2_dram.rearrange("(q s) d m -> s d q m", s=SB8)[s]).then_inc(x2q_in, 16)

            def chunk(c, first, last):
                if not first:
                    store_x2(c - 1, 3)
                    load_x2q(c - 1)
                    sp.wait_ge(x2q_in, 16 * SB8 * c)
                store_x2(c, 0)
                sp.wait_ge(ep_ready, c + 1)
                if not first:
                    sp.wait_ge(eblk_in, 16 * SB8 * c)
                sp.dma_start(e_dram, ep[:]).then_inc(ep_stored, 16)
                store_x2(c, 1)
                sp.wait_ge(ep_stored, 16 * c + 16)
                if not first:
                    sp.wait_ge(z3_done, c)
                for s in range(SB8):
                    sp.dma_start(eblk[s * D:(s + 1) * D, :, s * FG:(s + 1) * FG],
                                 e_dram.rearrange("(q s) d f -> s d q f", s=SB8)[s]).then_inc(eblk_in, 16)
                store_x2(c, 2)

            chunk(0, True, False)
            with sp.Fori(1, CHUNKS - 1) as c:
                chunk(c, False, False)
            chunk(CHUNKS - 1, False, True)
            store_x2(CHUNKS - 1, 3)
            load_x2q(CHUNKS - 1)
            sp.wait_ge(y_kept, CHUNKS)
            sp.dma_start(out, y_sb[:]).then_inc(y_out, 16)
            sp.wait_ge(y_out, 16)

        @block.gpsimd
        def _(pool):
            nc.gpsimd.memset(ident[:], 0.0).then_inc(ident_zero, 1)
            pool.wait_ge(ident_zero, 1)
            nc.gpsimd.affine_select(out=ident[:], in_=ident[:], compare_op=ALU.not_equal, fill=1.0, base=0,
                                    pattern=[[-1, P]], channel_multiplier=1).then_inc(ident_ok, 1)

            def gather(f):
                nc.gpsimd.indirect_dma_start(
                    out=e_next[:, f, :], out_offset=None, in_=tables[f],
                    in_offset=bass.IndirectOffsetOnAxis(ap=idx_cur[:, f:f + 1], axis=0)).then_inc(gathered, 16)

            pool.wait_ge(ids_in, 16)
            nc.gpsimd.tensor_copy(idx_cur[:], idx_all[:, 0, :]).then_inc(idx_ok, 1)
            pool.wait_ge(idx_ok, 1)
            for f in range(F):
                gather(f)

            def add(G, p, step, tt):
                n = 2 * 6 * p + 2 * step + tt
                tile = 2 * p + tt
                acc, y = lanes[:, tt, :], scaled
                if step < 4:
                    pool.wait_ge(act_scaled, SCALED * G + 10 * p + 2 * (step + 1) + tt + 1)
                if isinstance(G, int) and G == 0 and n < 2:
                    pass
                elif step == 0:
                    pool.wait_ge(pool_added, ADDS * G + n - 1)
                else:
                    pool.wait_ge(pool_added, ADDS * G + n - 1)
                if step == 0:
                    nc.gpsimd.tensor_tensor(acc, y[:, tt, :], y[:, 2 + tt, :], ALU.add).then_inc(pool_added, 1)
                elif step < 4:
                    w = NF[2 * step + 3] * M
                    nc.gpsimd.tensor_tensor(acc[:, 0:w], acc[:, 0:w], y[:, 2 * (step + 1) + tt, 0:w],
                                            ALU.add).then_inc(pool_added, 1)
                elif step == 4:
                    nc.gpsimd.tensor_tensor(acc[:, 0:2 * M], acc[:, 0:2 * M], acc[:, 2 * M:4 * M],
                                            ALU.add).then_inc(pool_added, 1)
                else:
                    return nc.gpsimd.tensor_tensor(xp[:, G_PAR[0], tile, :], acc[:, 0:M], acc[:, M:2 * M],
                                                   ALU.add).then_inc(pool_added, 1)

            G_PAR = [0]

            def chunk(c, first, last):
                if not last:
                    pool.wait_ge(gathered, 16 * F * (c + 1))
                    nc.gpsimd.tensor_copy(idx_cur[:], idx_all[:].rearrange("p c f -> p (c f)")
                                          [:, bass.ds((c + 1) * F, F)]).then_inc(idx_ok, 1)
                    pool.wait_ge(idx_ok, c + 2)
                    pool.wait_ge(e_dve_ok, c + 1)
                    pool.wait_ge(e_act_ok, c + 1)
                todo = [] if last else list(range(F))
                for gi in range(GROUPS):
                    G = 4 * c + gi
                    G_PAR[0] = gi % 2
                    for p in range(PAIRS):
                        for step in range(6):
                            if step == 5 and p == 0 and not (first and gi < 2):
                                pool.wait_ge(x2_ready, G - 1)
                            add(G, p, step, 0)
                            add(G, p, step, 1)
                            for f in todo[:2 if step == 0 else 1]:
                                gather(f)
                            del todo[:2 if step == 0 else 1]

            chunk(0, True, False)
            with pool.Fori(1, CHUNKS - 1) as c:
                chunk(c, False, False)
            chunk(CHUNKS - 1, False, True)

        @block.scalar
        def _(act):
            act.wait_ge(w0_sum, 1)
            nc.scalar.copy(w0h[0:ROWS[0], :], w0_s).then_inc(w0h_ok, 1)
            act.wait_ge(w1_in, 16)
            nc.scalar.copy(w1h[:], w1_raw).then_inc(w1h_ok, 1)

            def keep_pair_hi(n, t, slot, early):
                act.wait_ge(turned, n + 1)
                if not early:
                    act.wait_ge(l1_done, n - 1)
                r = ROWS[t]
                nc.scalar.copy(ph[0:r, slot, :], t_ps[0:r, slot, :]).then_inc(pair_hi, 1)

            def keep_x1_hi(G, par, early):
                act.wait_ge(l1_done, KT * (G + 1))
                if not early:
                    act.wait_ge(y_ready, UNITS * (G - 1))
                nc.scalar.copy(x1h[:, par, :], l1_ps[:]).then_inc(x1_hi, 1)

            def scale(G, gi, s, tt, first):
                p, j = s // 5, 2 * (s % 5) + 1
                tile, ja = 2 * p + tt, j // 2
                act.wait_ge(y_ready, UNITS * G + 4 * s + 2 + tt + 1)
                if not (first and gi == 0 and p == 0):
                    act.wait_ge(pool_added, ADDS * G + 12 * (p - 1) + 2 * max(0, ja - 1) + tt + 1)
                for i in range(NF[j]):
                    last = nc.scalar.activation(scaled[:, 2 * ja + tt, i * M:(i + 1) * M],
                                                l2_ps[:, 2 + tt, i * M:(i + 1) * M], ACT.Copy,
                                                scale=e_act[:, FPB * j + i, TPG * gi + tile:TPG * gi + tile + 1])
                last.then_inc(act_scaled, 1)

            def keep_g(c, q):
                act.wait_ge(g_done, QS * c + q + 1)
                nc.scalar.copy(gs[:].rearrange("p f b -> p b f")[:, SB8 * q:SB8 * (q + 1), :],
                               l3_ps[:, 0:SB8 * FG].rearrange("p (b f) -> p b f", f=FG)).then_inc(g_kept, 1)

            def keep_z3(c):
                act.wait_ge(z3_done, c + 1)
                nc.scalar.copy(z3t[:], l3_ps[:, 0:P]).then_inc(z3_ready, 1)

            for t in range(KT):
                keep_pair_hi(t, t, t % 2, t < 2)
            keep_x1_hi(0, 0, True)

            def chunk(c, first, last):
                act.wait_ge(gathered, 16 * F * (c + 1))
                if not first:
                    act.wait_ge(act_scaled, SCALED * GROUPS * c)
                nc.scalar.copy(e_act[:], e_next[:, 0:F, :]).then_inc(e_act_ok, 1)
                act.wait_ge(e_act_ok, c + 1)
                for gi in range(GROUPS):
                    G = 4 * c + gi
                    ahead = not (last and gi == GROUPS - 1)
                    if gi == 1:
                        act.wait_ge(filled, 4)
                        if not first:
                            act.wait_ge(ep_stored, 16 * c)
                        nc.scalar.copy(ep[:, :, 0:F], e_act[:].rearrange("p f d -> p d f")).then_inc(ep_ready, 1)
                    for s in range(SLOTS):
                        if ahead and 1 <= s <= KT:
                            keep_pair_hi(KT * (G + 1) + s - 1, s - 1, (KT * (gi + 1) + s - 1) % 2, False)
                        if ahead and s == KT + 1:
                            keep_x1_hi(G + 1, (gi + 1) % 2, first and gi == 0)
                        scale(G, gi, s, 0, first)
                        if gi == 1 and not first and s >= 2:
                            keep_g(c - 1, 2 * (s - 2))
                        if gi == 3 and not first and s == 1:
                            keep_z3(c - 1)
                        scale(G, gi, s, 1, first)
                        if gi == 1 and not first and s >= 2:
                            keep_g(c - 1, 2 * (s - 2) + 1)

            chunk(0, True, False)
            with act.Fori(1, CHUNKS - 1) as c:
                chunk(c, False, False)
            chunk(CHUNKS - 1, False, True)
            for q in range(QS):
                keep_g(CHUNKS - 1, q)
            keep_z3(CHUNKS - 1)

        @block.vector
        def _(dve):
            nc.vector.memset(ones_row[:], 1.0).then_inc(filled, 1)
            nc.vector.memset(dense_sb[:], 1.0).then_inc(filled, 1)
            nc.vector.memset(ep[:], 1.0).then_inc(filled, 1)
            nc.vector.memset(eblk[:], 0.0).then_inc(filled, 1)
            dve.wait_ge(w0_in, 32)
            nc.vector.tensor_tensor(w0_s, w0_a, w0_b, ALU.add).then_inc(w0_sum, 1)
            dve.wait_ge(w0h_ok, 1)
            nc.vector.tensor_tensor(w0l[0:ROWS[0], :], w0_s, w0h[0:ROWS[0], :].bitcast(F32),
                                    ALU.subtract).then_inc(w0l_ok, 1)
            dve.wait_ge(w1h_ok, 1)
            nc.vector.tensor_tensor(w1l[:], w1_raw, w1h[:].bitcast(F32), ALU.subtract).then_inc(w1l_ok, 1)

            def form_pairs(n, t, slot, gi, e, early):
                if not early:
                    dve.wait_ge(turned, n - 1)
                nk = ROWS[t] // F
                base = e[:]
                d0 = TPG * gi
                row = list(base.ap[0])
                left = bass.AP(tensor=base.tensor, offset=d0, ap=[row, [1, TPG], [0, nk], [D, F]])
                right = bass.AP(tensor=base.tensor, offset=d0 + KPT * t * D,
                                ap=[row, [1, TPG], [D, nk], [D, F]])
                nc.vector.tensor_tensor(
                    pairs[:, slot, :, 0:ROWS[t]].rearrange("p t (k f) -> p t k f", f=F),
                    left, right, ALU.mult).then_inc(pairs_ok, 1)

            def keep_pair_lo(n, t, slot):
                dve.wait_ge(pair_hi, n + 1)
                r = ROWS[t]
                nc.vector.tensor_tensor(pl[0:r, slot, :], t_ps[0:r, slot, :], ph[0:r, slot, :].bitcast(F32),
                                        ALU.subtract).then_inc(pair_lo, 1)

            def keep_x1_lo(G, gi, first):
                dve.wait_ge(x1_hi, G + 1)
                nc.vector.tensor_tensor(x1l[:, gi % 2, :], l1_ps[:], x1h[:, gi % 2, :].bitcast(F32),
                                        ALU.subtract).then_inc(x1_lo, 1)
                if gi == 0:
                    nc.vector.tensor_copy(z1acc[:], l1_ps[:]).then_inc(z1_added, 1)
                else:
                    dve.wait_ge(z1_added, G)
                    nc.vector.tensor_tensor(z1acc[:], l1_ps[:], z1acc[:], ALU.add).then_inc(z1_added, 1)

            def fma(G, gi, s, i, tt, first):
                p, j = s // 5, 2 * (s % 5)
                tile, f = 2 * p + tt, FPB * j + i
                n = FMAS // 2 * p + 8 * (s % 5) + 2 * i + tt
                if i == 0:
                    dve.wait_ge(y_ready, UNITS * G + 4 * s + tt + 1)
                e_col = e_dve[:, f, TPG * gi + tile:TPG * gi + tile + 1]
                y = l2_ps[:, tt, i * M:(i + 1) * M]
                acc = xd[:, gi % 2, tile, :]
                if f == 0:
                    nc.vector.tensor_scalar(acc, y, e_col, None, ALU.mult).then_inc(fma_done, 1)
                else:
                    dve.wait_ge(fma_done, FMAS * G + n - 1)
                    nc.vector.scalar_tensor_tensor(out=acc, in0=y, scalar=e_col, in1=acc, op0=ALU.mult,
                                                   op1=ALU.add).then_inc(fma_done, 1)

            def join_x2(G, par):
                dve.wait_ge(fma_done, FMAS * (G + 1))
                dve.wait_ge(pool_added, ADDS * (G + 1))
                nc.vector.tensor_tensor(xd[:, par], xd[:, par], xp[:, par], ALU.add).then_inc(x2_ready, 1)

            def fold_z1(c, first):
                dve.wait_ge(z1_added, GROUPS * (c + 1))
                if not first:
                    dve.wait_ge(h1_done, c)
                nc.vector.tensor_tensor(z1half[:], z1acc[:, 0:2 * P], z1acc[:, 2 * P:4 * P],
                                        ALU.add).then_inc(z1_fold, 1)
                dve.wait_ge(z1_fold, 2 * c + 1)
                nc.vector.tensor_tensor(z1t[:], z1half[:, 0:P], z1half[:, P:2 * P], ALU.add).then_inc(z1_fold, 1)
                dve.wait_ge(z1_fold, 2 * c + 2)

            def relu_h1(c):
                dve.wait_ge(h1_done, c + 1)
                nc.vector.tensor_scalar(h1s[:], l3_ps[:], 0.0, None, ALU.max).then_inc(h1_ready, 1)

            def relu_h2(c):
                dve.wait_ge(h2_done, c + 1)
                nc.vector.tensor_scalar(h2s[:], l3_ps[:, 0:H2], 0.0, None, ALU.max).then_inc(h2_ready, 1)

            def keep_y(c):
                dve.wait_ge(y_done, c + 1)
                nc.vector.tensor_scalar(y_sb[:, bass.ds(c * P, P)], l3_ps[0:1, 0:P], 1.0, None,
                                        ALU.mult).then_inc(y_kept, 1)

            def wrap_e(c):
                dve.wait_ge(gathered, 16 * F * (c + 1))
                nc.vector.tensor_copy(e_next[:, F:FX, :], e_next[:, 0:FX - F, :]).then_inc(e_wrapped, 1)
                dve.wait_ge(e_wrapped, c + 1)

            wrap_e(0)
            form_pairs(0, 0, 0, 0, e_next, True)
            for t in range(KT):
                if t + 1 < KT:
                    form_pairs(t + 1, t + 1, (t + 1) % 2, 0, e_next, t + 1 < 2)
                keep_pair_lo(t, t, t % 2)
            keep_x1_lo(0, 0, True)

            def chunk(c, first, last):
                if not first:
                    dve.wait_ge(fma_done, FMAS * GROUPS * c)
                nc.vector.tensor_copy(e_dve[:], e_next[:]).then_inc(e_dve_ok, 1)
                dve.wait_ge(e_dve_ok, c + 1)
                for gi in range(GROUPS):
                    G = 4 * c + gi
                    ahead = not (last and gi == GROUPS - 1)
                    late = not first
                    if gi == GROUPS - 1 and ahead:
                        wrap_e(c + 1)
                    if not (first and gi < 2):
                        dve.wait_ge(x2_stored, 16 * (G - 1))
                    for s in range(SLOTS):
                        if ahead and s < KT:
                            form_pairs(KT * (G + 1) + s, s, (KT * (gi + 1) + s) % 2, (gi + 1) % GROUPS,
                                       e_next if gi == GROUPS - 1 else e_dve, False)
                        if ahead and s == KT + 1:
                            keep_x1_lo(G + 1, (gi + 1) % GROUPS, first)
                        for i in range(FPB):
                            for tt in range(2):
                                fma(G, gi, s, i, tt, first)
                            if i == 1 and ahead and 1 <= s <= KT:
                                keep_pair_lo(KT * (G + 1) + s - 1, s - 1, (KT * (gi + 1) + s - 1) % 2)
                        if s == 3 and not (first and gi == 0):
                            join_x2(G - 1, (gi - 1) % 2)
                        if gi == 3 and s == 6:
                            if late:
                                relu_h1(c - 1)
                            fold_z1(c, first)
                        if gi == 3 and s == 8 and late:
                            relu_h2(c - 1)
                if not first:
                    keep_y(c - 1)

            chunk(0, True, False)
            with dve.Fori(1, CHUNKS - 1) as c:
                chunk(c, False, False)
            chunk(CHUNKS - 1, False, True)
            end = CHUNKS - 1
            join_x2(4 * end + 3, 1)
            relu_h1(end)
            relu_h2(end)
            keep_y(end)

        @block.tensor
        def _(pe):
            def turn_pairs(n, t, slot, early):
                pe.wait_ge(pairs_ok, n + 1)
                if not early:
                    pe.wait_ge(pair_lo, n - 1)
                r = ROWS[t]
                for k in range(TPG):
                    last = nc.tensor.transpose(t_ps[0:r, slot, k * P:(k + 1) * P], pairs[:, slot, k, 0:r], ident[:])
                last.then_inc(turned, 1)

            def contract_pairs(n, t, slot):
                pe.wait_ge(pair_lo, n + 1)
                r = ROWS[t]
                w = slice(t * M, (t + 1) * M)
                nc.tensor.matmul(l1_ps[:], w0h[0:r, w], ph[0:r, slot, :], start=(t == 0), stop=False)
                nc.tensor.matmul(l1_ps[:], w0h[0:r, w], pl[0:r, slot, :], start=False, stop=False)
                nc.tensor.matmul(l1_ps[:], w0l[0:r, w], ph[0:r, slot, :], start=False,
                                 stop=(t == KT - 1)).then_inc(l1_done, 1)

            def layer2(G, gi, u, first):
                p, j, tt = u // 20, (u % 20) // 2, u % 2
                if not (first and gi == 0 and u < 4):
                    if j % 2 == 0:
                        pe.wait_ge(fma_done, FMAS * G + FMAS // 2 * p + 4 * j - 1 + tt)
                    else:
                        pe.wait_ge(act_scaled, SCALED * G + 10 * p + j - 2 + tt)
                cols = slice((2 * p + tt) * P, (2 * p + tt + 1) * P)
                rows = slice(FPB * j * M, (FPB * j + NF[j]) * M)
                y = l2_ps[:, u % 4, 0:NF[j] * M]
                xh, xl = x1h[:, gi % 2, cols], x1l[:, gi % 2, cols]
                nc.tensor.matmul(y, xh, w1h[:, rows], start=True, stop=False)
                nc.tensor.matmul(y, xh, w1l[:, rows], start=False, stop=False)
                nc.tensor.matmul(y, xl, w1h[:, rows], start=False, stop=True).then_inc(y_ready, 1)

            def layer3_g(c, q, one_bank=True):
                if q == 0:
                    pe.wait_ge(x2q_in, 16 * SB8 * (c + 1))
                    pe.wait_ge(eblk_in, 16 * SB8 * (c + 1))
                else:
                    pe.wait_ge(g_kept, QS * c + q)
                nc.tensor.matmul(l3_ps[:, 0:SB8 * FG], x2q[:, q, :], eblk[:, q, :], start=True,
                                 stop=True).then_inc(g_done, 1)

            def layer3_f(c, f):
                if f == 0:
                    pe.wait_ge(g_kept, QS * (c + 1))
                mm = nc.tensor.matmul(l3_ps[:, 0:P], w2[:, f, :], gs[:, f, :], start=(f == 0), stop=(f == F - 1))
                if f == F - 1:
                    mm.then_inc(z3_done, 1)

            def mlp1(c, m):
                if m == 0:
                    pe.wait_ge(z3_ready, c + 1)
                    pe.wait_ge(z1_fold, 2 * (c + 1))
                cols = slice(m * P, (m + 1) * P)
                for k, z in enumerate((z1t[:], gs[:, F, :], z3t[:])):
                    nc.tensor.matmul(l3_ps[:, cols], wt1[:, k, cols], z, start=(k == 0), stop=False)
                mm = nc.tensor.matmul(l3_ps[:, cols], wtd[:, cols], dense_sb[:, bass.ds(c * P, P)], start=False, stop=True)
                if m == H1 // P - 1:
                    mm.then_inc(h1_done, 1)

            def mlp2(c, m):
                if m == 0:
                    pe.wait_ge(h1_ready, c + 1)
                cols = slice(m * P, (m + 1) * P)
                for k in range(H1 // P):
                    nc.tensor.matmul(l3_ps[:, cols], wt2[:, k, cols], h1s[:, k * P:(k + 1) * P],
                                     start=(k == 0), stop=False)
                mm = nc.tensor.matmul(l3_ps[:, cols], bt2[:, cols], ones_row[:], start=False, stop=True)
                if m == H2 // P - 1:
                    mm.then_inc(h2_done, 1)

            def mlp3(c):
                pe.wait_ge(h2_ready, c + 1)
                for k in range(H2 // P):
                    mm = nc.tensor.matmul(l3_ps[0:1, 0:P], wt3[:, k:k + 1], h2s[:, k * P:(k + 1) * P],
                                          start=(k == 0), stop=(k == H2 // P - 1))
                mm.then_inc(y_done, 1)

            pe.wait_ge(ident_ok, 1)
            pe.wait_ge(w0h_ok, 1)
            pe.wait_ge(w0l_ok, 1)
            turn_pairs(0, 0, 0, True)
            for t in range(KT):
                if t + 1 < KT:
                    turn_pairs(t + 1, t + 1, (t + 1) % 2, t + 1 < 2)
                contract_pairs(t, t, t % 2)
            pe.wait_ge(w1l_ok, 1)
            pe.wait_ge(w2_in, 16)
            pe.wait_ge(top_in, 96)
            pe.wait_ge(filled, 4)
            pe.wait_ge(dense_in, 16)

            def chunk(c, first, last):
                for gi in range(GROUPS):
                    G = 4 * c + gi
                    ahead = not (last and gi == GROUPS - 1)
                    pe.wait_ge(x1_lo, G + 1)
                    for s in range(SLOTS):
                        for v in range(4):
                            u = 4 * s + v
                            layer2(G, gi, u, first)
                            if first:
                                continue
                            if gi == 1 and s >= 2 and v % 2 == 1:
                                layer3_g(c - 1, 2 * (s - 2) + v // 2)
                            if gi == 2 and u < F:
                                layer3_f(c - 1, u)
                            if gi == 3 and v == 3 and 2 <= s < 2 + H1 // P:
                                mlp1(c - 1, s - 2)
                            if gi == 3 and v == 3 and 7 <= s < 7 + H2 // P:
                                mlp2(c - 1, s - 7)
                        if ahead and 1 <= s <= KT:
                            if s == 1:
                                pe.wait_ge(z1_added, G + 1)
                            contract_pairs(KT * (G + 1) + s - 1, s - 1, (KT * (gi + 1) + s - 1) % 2)
                        if ahead and s < KT:
                            turn_pairs(KT * (G + 1) + s, s, (KT * (gi + 1) + s) % 2, False)
                if not first:
                    mlp3(c - 1)

            chunk(0, True, False)
            with pe.Fori(1, CHUNKS - 1) as c:
                chunk(c, False, False)
            chunk(CHUNKS - 1, False, True)
            end = CHUNKS - 1
            for q in range(QS):
                layer3_g(end, q)
            for f in range(F):
                layer3_f(end, f)
            for m in range(H1 // P):
                mlp1(end, m)
            for m in range(H2 // P):
                mlp2(end, m)
            mlp3(end)


def kernel(**inputs):
    import concourse.bacc as _bacc
    from concourse.bass_utils import run_bass_kernel_spmd as _run

    f0 = np.asarray(inputs["L0_rec_f0"])
    a, b = pair_rows()
    w0 = np.zeros((2, KT * KPT * F, M), f0.dtype)
    w0[0, :a.size] = f0[a]
    w0[1, F:b.size] = f0[b[F:]]
    w0 = np.ascontiguousarray(w0.reshape(2, KT, KPT * F, M).transpose(0, 2, 1, 3)).reshape(2, KPT * F, KT * M)
    arrays = {"ids": np.ascontiguousarray(inputs["ids"])}
    for f in range(F):
        arrays[f"tbl_{f}"] = np.ascontiguousarray(inputs[f"tbl_{f}"])
    arrays["w0a"], arrays["w0b"] = np.ascontiguousarray(w0[0]), np.ascontiguousarray(w0[1])
    for name, key in (("f1", "L0_rec_f1"), ("f2", "L0_rec_f2"), ("wt1", "W_top1"), ("wt2", "W_top2")):
        arrays[name] = np.ascontiguousarray(inputs[key])
    arrays["wt3"] = np.ascontiguousarray(np.asarray(inputs["W_top3"]).reshape(H2 // P, P).T)
    arrays["bt1"] = np.ascontiguousarray(inputs["b_top1"]).reshape(1, H1)
    arrays["bt2"] = np.ascontiguousarray(inputs["b_top2"]).reshape(1, H2)
    arrays["dense_t"] = np.ascontiguousarray(np.asarray(inputs["dense_ctx"]).T)

    nc = _bacc.Bacc("TRN2", target_bir_lowering=False, num_devices=1)
    ap = {k: nc.dram_tensor(f"in_{k}", v.shape, mybir.dt.from_np(v.dtype), kind="ExternalInput").ap()
          for k, v in arrays.items()}
    out = nc.dram_tensor("out_y", (1, B), F32, kind="ExternalOutput").ap()
    build(nc, ap["ids"], [ap[f"tbl_{f}"] for f in range(F)], ap["w0a"], ap["w0b"], ap["f1"], ap["f2"],
          ap["wt1"], ap["bt1"], ap["wt2"], ap["bt2"], ap["wt3"], ap["dense_t"], out)
    r = _run(nc, [{f"in_{k}": v for k, v in arrays.items()}], core_ids=[0])
    return r.results[0]["out_y"].reshape(B, 1)
```

```python
from contextlib import ExitStack

import numpy as np
import concourse.bass as bass
from concourse import mybir

F32 = mybir.dt.float32
F32R = mybir.dt.float32r
I32 = mybir.dt.int32
ALU = mybir.AluOpType
ACT = mybir.ActivationFunctionType

P = 128
B, F, D, M = 512, 39, 16, 128
CHUNKS = B // P
TPG = 4
GROUPS = D // TPG
COLS = TPG * P
NK = F // 2 + 1
KPT = P // F
KT = -(-NK // KPT)
ROWS = [F * min(KPT, NK - KPT * t) for t in range(KT)]
FPB = 4
BLOCKS = -(-F // FPB)
NF = [min(FPB, F - FPB * j) for j in range(BLOCKS)]
PAIRS = TPG // 2
UNITS = TPG * BLOCKS
FMAS = TPG * FPB * BLOCKS // 2
SCALED = TPG * BLOCKS // 2
ADDS = PAIRS * 2 * (BLOCKS // 2 + 1)
SLOTS = BLOCKS
SB8 = P // D
QS = P // SB8
FG = F + 1
H1, H2 = 512, 256
ZT = 3
DENSE = 16
G_SLOT, F_SLOT = 7, 15


def pair_rows():
    k = np.arange(NK)[:, None]
    f = np.arange(F)[None, :]
    g = (f + k) % F
    return (f * F + g).reshape(-1), (g * F + f).reshape(-1)


def build(nc, ids, tables, w0a_d, w0b_d, f1, f2, wt1_d, bt1_d, wt2_d, bt2_d, wt3_d, dense_t, out):
    ctx = ExitStack()
    with ctx:
        def sb(name, shape, dt=F32):
            return ctx.enter_context(nc.sbuf_tensor(name, shape, dt))

        def sem(name):
            return ctx.enter_context(nc.semaphore(name))

        w1h = sb("w1h", [P, F * M], F32R)
        w1l = sb("w1l", [P, F * M], F32R)
        w0h = sb("w0h", [P, KT * M], F32R)
        w0l = sb("w0l", [P, KT * M], F32R)
        w2 = sb("w2", [P, F, M])
        wt1 = sb("wt1", [P, ZT, H1])
        wtd = sb("wtd", [DENSE + 1, H1])
        wt2 = sb("wt2", [P, H1 // P, H2])
        bt2 = sb("bt2", [1, H2])
        wt3 = sb("wt3", [P, H2 // P])
        ident = sb("ident", [P, P])
        ones_row = sb("ones_row", [1, P])
        idx_all = sb("idx_all", [P, CHUNKS, F], I32)
        idx_cur = sb("idx_cur", [P, F], I32)
        e_next = sb("e_next", [P, F, D])
        e_cur = sb("e_cur", [P, F, D])
        ep = sb("ep", [P, D, FG])
        tripled = sb("tripled", [P, TPG, KPT, F])
        turned = sb("turned", [KPT * F, COLS])
        shifted = sb("shifted", [KPT * F, KT, COLS])
        ph = sb("ph", [P, 2, COLS], F32R)
        pl = sb("pl", [P, 2, COLS], F32R)
        x1h = sb("x1h", [P, 2, COLS], F32R)
        x1l = sb("x1l", [P, 2, COLS], F32R)
        scaled = sb("scaled", [P, BLOCKS, FPB * M])
        xd = sb("xd", [P, 2, TPG, M])
        xp = sb("xp", [P, 2, TPG, M])
        z1acc = sb("z1acc", [P, COLS])
        z1t = sb("z1t", [P, P])
        x2q = sb("x2q", [P, QS, M])
        eblk = sb("eblk", [P, QS, SB8 * FG])
        gs = sb("gs", [P, FG, P])
        z3t = sb("z3t", [P, P])
        dense_sb = sb("dense_sb", [DENSE + 1, B])
        h1s = sb("h1s", [P, H1])
        h2s = sb("h2s", [P, H2])
        y_sb = sb("y_sb", [1, B])

        w1_raw = gs[:].rearrange("p f b -> p (f b)")[:, 0:F * M]
        raw = scaled[:].rearrange("p s n -> p (s n)")
        w0_a, w0_b, w0_s = (raw[0:ROWS[0], n * KT * M:(n + 1) * KT * M] for n in range(3))

        l2_ps = ctx.enter_context(nc.psum_tensor("l2_ps", [P, 4, 512], F32))
        turn_ps = ctx.enter_context(nc.psum_tensor("turn_ps", [P, 512], F32))
        pair_ps = ctx.enter_context(nc.psum_tensor("pair_ps", [P, 512], F32))
        l1_ps = ctx.enter_context(nc.psum_tensor("l1_ps", [P, 512], F32))
        l3_ps = ctx.enter_context(nc.psum_tensor("l3_ps", [P, 512], F32))

        x2_dram = nc.dram_tensor("x2_dram", [P, D, M], F32, kind="Internal").ap()
        e_dram = nc.dram_tensor("e_dram", [P, D, FG], F32, kind="Internal").ap()

        ids_in, w0_in, w1_in, w2_in, top_in = (sem(n) for n in ("ids_in", "w0_in", "w1_in", "w2_in", "top_in"))
        w0_sum, w0h_ok, w0l_ok, w1h_ok, w1l_ok = (sem(n) for n in ("w0_sum", "w0h_ok", "w0l_ok", "w1h_ok", "w1l_ok"))
        ident_zero, ident_ok, filled = sem("ident_zero"), sem("ident_ok"), sem("filled")
        idx_ok, gathered, e_cur_ok = sem("idx_ok"), sem("gathered"), sem("e_cur_ok")
        tripled_ok = sem("tripled_ok")
        turned_ps = sem("turned_ps")
        turned_ok = sem("turned_ok")
        shifted_in = [sem(f"shifted_in{t}") for t in range(KT)]
        pairs_ok = sem("pairs_ok")
        pair_hi = sem("pair_hi")
        pair_lo = sem("pair_lo")
        l1_done = sem("l1_done")
        x1_hi, x1_lo, z1_added = sem("x1_hi"), sem("x1_lo"), sem("z1_added")
        y_ready = sem("y_ready")
        fma_done = sem("fma_done")
        act_scaled = sem("act_scaled")
        pool_added = sem("pool_added")
        x2_ready, x2_stored, x2q_in = sem("x2_ready"), sem("x2_stored"), sem("x2q_in")
        ep_ready, ep_stored, eblk_in = sem("ep_ready"), sem("ep_stored"), sem("eblk_in")
        g_done, g_kept, z3_done, z3_ready = sem("g_done"), sem("g_kept"), sem("z3_done"), sem("z3_ready")
        z1_fold, dense_in = sem("z1_fold"), sem("dense_in")
        h1_done, h1_ready, h2_done, h2_ready = sem("h1_done"), sem("h1_ready"), sem("h2_done"), sem("h2_ready")
        y_done, y_kept, y_out = sem("y_done"), sem("y_kept"), sem("y_out")

        block = ctx.enter_context(nc.Block())

        @block.sync
        def _(sp):
            sp.dma_start(idx_all[:], ids.rearrange("(c p) f -> p c f", p=P)).then_inc(ids_in, 16)
            sp.dma_start(w0_a, w0a_d).then_inc(w0_in, 16)
            sp.dma_start(w0_b, w0b_d).then_inc(w0_in, 16)
            sp.dma_start(w1_raw.rearrange("p (f m) -> p f m", m=M),
                         f1.rearrange("(f g) m -> g f m", g=M)).then_inc(w1_in, 16)
            sp.dma_start(w2[:], f2.rearrange("(f g) m -> g f m", g=M)).then_inc(w2_in, 16)
            sp.dma_start(wt1[:], wt1_d[0:ZT * P, :].rearrange("(k p) n -> p k n", p=P)).then_inc(top_in, 16)
            sp.dma_start(wtd[0:DENSE, :], wt1_d[ZT * P:ZT * P + DENSE, :]).then_inc(top_in, 16)
            sp.dma_start(wtd[DENSE:DENSE + 1, :], bt1_d).then_inc(top_in, 16)
            sp.dma_start(wt2[:], wt2_d.rearrange("(k p) n -> p k n", p=P)).then_inc(top_in, 16)
            sp.dma_start(bt2[:], bt2_d).then_inc(top_in, 16)
            sp.dma_start(wt3[:], wt3_d).then_inc(top_in, 16)
            sp.wait_ge(filled, 4)
            sp.dma_start(dense_sb[0:DENSE, :], dense_t).then_inc(dense_in, 16)

            def shift(G, first):
                sp.wait_ge(turned_ok, G + 1)
                for t in range(KT):
                    if not first:
                        sp.wait_ge(pairs_ok, KT * (G - 1) + t + 1)
                    for j in range(ROWS[t] // F):
                        k = KPT * t + j
                        sp.dma_start(shifted[j * F:(j + 1) * F, t, :],
                                     turned[k:k + F, :]).then_inc(shifted_in[t], 16)

            def store_x2(c, gi):
                sp.wait_ge(x2_ready, 4 * c + gi + 1)
                sp.dma_start(x2_dram[:, TPG * gi:TPG * gi + TPG, :],
                             xd[:, gi % 2]).then_inc(x2_stored, 16)

            def load_x2q(c):
                sp.wait_ge(x2_stored, 64 * (c + 1))
                for s in range(SB8):
                    sp.dma_start(x2q[s * D:(s + 1) * D, :, :],
                                 x2_dram.rearrange("(q s) d m -> s d q m", s=SB8)[s]).then_inc(x2q_in, 16)

            def chunk(c, first, last):
                for gi in range(GROUPS):
                    if not (last and gi == GROUPS - 1):
                        shift(4 * c + gi + 1, False)
                    if gi == 0 and not first:
                        store_x2(c - 1, 3)
                        load_x2q(c - 1)
                    if gi == 1:
                        if not first:
                            sp.wait_ge(x2q_in, 16 * SB8 * c)
                        store_x2(c, 0)
                        sp.wait_ge(ep_ready, c + 1)
                        if not first:
                            sp.wait_ge(eblk_in, 16 * SB8 * c)
                        sp.dma_start(e_dram, ep[:]).then_inc(ep_stored, 16)
                    if gi == 2:
                        store_x2(c, 1)
                        sp.wait_ge(ep_stored, 16 * c + 16)
                        if not first:
                            sp.wait_ge(z3_done, c)
                        for s in range(SB8):
                            sp.dma_start(eblk[s * D:(s + 1) * D, :, s * FG:(s + 1) * FG],
                                         e_dram.rearrange("(q s) d f -> s d q f", s=SB8)[s]).then_inc(eblk_in, 16)
                    if gi == 3:
                        store_x2(c, 2)

            shift(0, True)
            chunk(0, True, False)
            with sp.Fori(1, CHUNKS - 1) as c:
                chunk(c, False, False)
            chunk(CHUNKS - 1, False, True)
            store_x2(CHUNKS - 1, 3)
            load_x2q(CHUNKS - 1)
            sp.wait_ge(y_kept, CHUNKS)
            sp.dma_start(out, y_sb[:]).then_inc(y_out, 16)
            sp.wait_ge(y_out, 16)

        @block.gpsimd
        def _(pool):
            nc.gpsimd.memset(ident[:], 0.0).then_inc(ident_zero, 1)
            pool.wait_ge(ident_zero, 1)
            nc.gpsimd.affine_select(out=ident[:], in_=ident[:], compare_op=ALU.not_equal, fill=1.0, base=0,
                                    pattern=[[-1, P]], channel_multiplier=1).then_inc(ident_ok, 1)

            def gather(f):
                nc.gpsimd.indirect_dma_start(
                    out=e_next[:, f, :], out_offset=None, in_=tables[f],
                    in_offset=bass.IndirectOffsetOnAxis(ap=idx_cur[:, f:f + 1], axis=0)).then_inc(gathered, 16)

            pool.wait_ge(ids_in, 16)
            nc.gpsimd.tensor_copy(idx_cur[:], idx_all[:, 0, :]).then_inc(idx_ok, 1)
            pool.wait_ge(idx_ok, 1)
            for f in range(F):
                gather(f)

            def add(G, gi, p, step, tt):
                n = 12 * p + 2 * step + tt
                if step < 4:
                    pool.wait_ge(act_scaled, SCALED * G + 10 * p + 2 * (step + 1) + tt + 1)
                if step > 0:
                    pool.wait_ge(pool_added, ADDS * G + n - 1)
                s = [scaled[:, 2 * ja + tt, :] for ja in range(5)]
                if step < 3:
                    nc.gpsimd.tensor_tensor(s[step + 1], s[step], s[step + 1], ALU.add).then_inc(pool_added, 1)
                elif step == 3:
                    w = NF[-1 - BLOCKS % 2] * M
                    nc.gpsimd.tensor_tensor(s[3][:, 0:w], s[3][:, 0:w], s[4][:, 0:w],
                                            ALU.add).then_inc(pool_added, 1)
                elif step == 4:
                    nc.gpsimd.tensor_tensor(s[3][:, 0:2 * M], s[3][:, 0:2 * M], s[3][:, 2 * M:4 * M],
                                            ALU.add).then_inc(pool_added, 1)
                else:
                    nc.gpsimd.tensor_tensor(xp[:, gi % 2, 2 * p + tt, :], s[3][:, 0:M], s[3][:, M:2 * M],
                                            ALU.add).then_inc(pool_added, 1)

            def chunk(c, first, last):
                if not last:
                    pool.wait_ge(gathered, 16 * F * (c + 1))
                    nc.gpsimd.tensor_copy(idx_cur[:], idx_all[:].rearrange("p c f -> p (c f)")
                                          [:, bass.ds((c + 1) * F, F)]).then_inc(idx_ok, 1)
                    pool.wait_ge(idx_ok, c + 2)
                    pool.wait_ge(e_cur_ok, c + 1)
                    pool.wait_ge(ep_ready, c + 1)
                    pool.wait_ge(tripled_ok, GROUPS * c + 2)
                todo = [] if last else list(range(F))
                for gi in range(GROUPS):
                    G = 4 * c + gi
                    for p in range(PAIRS):
                        for step in range(6):
                            if step == 5 and p == 0 and not (first and gi < 2):
                                pool.wait_ge(x2_ready, G - 1)
                            add(G, gi, p, step, 0)
                            add(G, gi, p, step, 1)
                            for f in todo[:2 if step == 0 else 1]:
                                gather(f)
                            del todo[:2 if step == 0 else 1]

            chunk(0, True, False)
            with pool.Fori(1, CHUNKS - 1) as c:
                chunk(c, False, False)
            chunk(CHUNKS - 1, False, True)

        @block.scalar
        def _(act):
            act.wait_ge(w0_sum, 1)
            nc.scalar.copy(w0h[0:ROWS[0], :], w0_s).then_inc(w0h_ok, 1)
            act.wait_ge(w1_in, 16)
            nc.scalar.copy(w1h[:], w1_raw).then_inc(w1h_ok, 1)

            def triple(G, gi, e):
                if not (isinstance(G, int) and G == 0):
                    act.wait_ge(turned_ps, G)
                base = e[:, TPG * gi:TPG * gi + TPG, 0:F]
                rep = bass.AP(tensor=base.tensor, offset=base.offset,
                              ap=[list(base.ap[0]), list(base.ap[1]), [0, KPT], list(base.ap[2])])
                nc.scalar.copy(tripled[:], rep).then_inc(tripled_ok, 1)

            def keep_turned(G):
                act.wait_ge(turned_ps, G + 1)
                if not (isinstance(G, int) and G == 0):
                    act.wait_ge(pairs_ok, KT * G)
                nc.scalar.copy(turned[:], turn_ps[0:KPT * F, :]).then_inc(turned_ok, 1)

            def keep_pair_hi(n, t, slot, bank, early):
                act.wait_ge(pairs_ok, n + 1)
                if not early:
                    act.wait_ge(l1_done, n - 1)
                r = ROWS[t]
                nc.scalar.copy(ph[0:r, slot, :], bank[0:r, :]).then_inc(pair_hi, 1)

            def keep_x1_hi(G, par, early):
                act.wait_ge(l1_done, KT * (G + 1))
                if not early:
                    act.wait_ge(y_ready, UNITS * (G - 1))
                nc.scalar.copy(x1h[:, par, :], l1_ps[:]).then_inc(x1_hi, 1)

            def scale(G, gi, s, tt, first):
                p, j = s // 5, 2 * (s % 5) + 1
                tile, ja = 2 * p + tt, j // 2
                act.wait_ge(y_ready, UNITS * G + 4 * s + 2 + tt + 1)
                if not (first and gi == 0 and p == 0):
                    free = (0, 1, 2, 5, 3)[ja]
                    act.wait_ge(pool_added, ADDS * G + 12 * (p - 1) + 2 * free + tt + 1)
                for i in range(NF[j]):
                    last = nc.scalar.activation(scaled[:, 2 * ja + tt, i * M:(i + 1) * M],
                                                l2_ps[:, 2 + tt, i * M:(i + 1) * M], ACT.Copy,
                                                scale=ep[:, TPG * gi + tile, FPB * j + i:FPB * j + i + 1])
                last.then_inc(act_scaled, 1)

            def keep_g(c, q, bank):
                act.wait_ge(g_done, QS * c + q + 1)
                nc.scalar.copy(gs[:].rearrange("p f b -> p b f")[:, SB8 * q:SB8 * (q + 1), :],
                               bank[:, 0:SB8 * FG].rearrange("p (b f) -> p b f", f=FG)).then_inc(g_kept, 1)

            def keep_z3(c):
                act.wait_ge(z3_done, c + 1)
                nc.scalar.copy(z3t[:], l3_ps[:, 0:P]).then_inc(z3_ready, 1)

            e_turned = e_next[:].rearrange("p f d -> p d f")

            act.wait_ge(gathered, 16 * F)
            triple(0, 0, e_turned)
            keep_turned(0)
            triple(1, 1, e_turned)
            for t in range(KT):
                keep_pair_hi(t, t, t % 2, l2_ps[:, t % 4, :], t < 2)
            keep_x1_hi(0, 0, True)

            def chunk(c, first, last):
                if first:
                    act.wait_ge(filled, 4)
                else:
                    act.wait_ge(act_scaled, SCALED * GROUPS * c)
                    act.wait_ge(ep_stored, 16 * c)
                nc.scalar.copy(ep[:, :, 0:F], e_next[:].rearrange("p f d -> p d f")).then_inc(ep_ready, 1)
                act.wait_ge(ep_ready, c + 1)
                for gi in range(GROUPS):
                    G = 4 * c + gi
                    ahead = not (last and gi == GROUPS - 1)
                    for s in range(SLOTS):
                        if ahead and s == 0:
                            keep_turned(G + 1)
                        if ahead and 1 <= s <= KT:
                            keep_pair_hi(KT * (G + 1) + s - 1, s - 1, (KT * (gi + 1) + s - 1) % 2, pair_ps, False)
                        if ahead and s == KT + 1:
                            keep_x1_hi(G + 1, (gi + 1) % 2, first and gi == 0)
                        q = 2 * (SLOTS * gi + s - G_SLOT)
                        if not first and 0 <= q < QS:
                            keep_g(c - 1, q, l3_ps)
                        scale(G, gi, s, 0, first)
                        scale(G, gi, s, 1, first)
                        if not first and 0 <= q < QS:
                            keep_g(c - 1, q + 1, l3_ps)
                        if gi == 2 and not first and s == SLOTS - 1:
                            keep_z3(c - 1)
                    if gi < 2:
                        triple(G + 2, gi + 2, ep)
                    elif not last:
                        if gi == 2:
                            act.wait_ge(gathered, 16 * F * (c + 2))
                        triple(G + 2, gi - 2, e_turned)

            chunk(0, True, False)
            with act.Fori(1, CHUNKS - 1) as c:
                chunk(c, False, False)
            chunk(CHUNKS - 1, False, True)
            for q in range(QS):
                keep_g(CHUNKS - 1, q, l2_ps[:, q % 4, :])
            keep_z3(CHUNKS - 1)

        @block.vector
        def _(dve):
            nc.vector.memset(ones_row[:], 1.0).then_inc(filled, 1)
            nc.vector.memset(dense_sb[:], 1.0).then_inc(filled, 1)
            nc.vector.memset(ep[:], 1.0).then_inc(filled, 1)
            nc.vector.memset(eblk[:], 0.0).then_inc(filled, 1)
            dve.wait_ge(w0_in, 32)
            nc.vector.tensor_tensor(w0_s, w0_a, w0_b, ALU.add).then_inc(w0_sum, 1)
            dve.wait_ge(w0h_ok, 1)
            nc.vector.tensor_tensor(w0l[0:ROWS[0], :], w0_s, w0h[0:ROWS[0], :].bitcast(F32),
                                    ALU.subtract).then_inc(w0l_ok, 1)
            dve.wait_ge(w1h_ok, 1)
            nc.vector.tensor_tensor(w1l[:], w1_raw, w1h[:].bitcast(F32), ALU.subtract).then_inc(w1l_ok, 1)

            def form_pairs(n, t, G, bank, kept):
                if not (isinstance(kept, int) and kept < 1):
                    dve.wait_ge(pair_lo, kept)
                dve.wait_ge(shifted_in[t], 16 * (ROWS[t] // F) * (G + 1))
                r = ROWS[t]
                nc.vector.tensor_tensor(bank[0:r, :], turn_ps[0:r, :], shifted[0:r, t, :],
                                        ALU.mult).then_inc(pairs_ok, 1)

            def keep_pair_lo(n, t, slot, bank):
                dve.wait_ge(pair_hi, n + 1)
                r = ROWS[t]
                nc.vector.tensor_tensor(pl[0:r, slot, :], bank[0:r, :], ph[0:r, slot, :].bitcast(F32),
                                        ALU.subtract).then_inc(pair_lo, 1)

            def keep_x1_lo(G, gi, first):
                dve.wait_ge(x1_hi, G + 1)
                nc.vector.tensor_tensor(x1l[:, gi % 2, :], l1_ps[:], x1h[:, gi % 2, :].bitcast(F32),
                                        ALU.subtract).then_inc(x1_lo, 1)
                if gi == 0:
                    nc.vector.tensor_copy(z1acc[:], l1_ps[:]).then_inc(z1_added, 1)
                else:
                    dve.wait_ge(z1_added, G)
                    nc.vector.tensor_tensor(z1acc[:], l1_ps[:], z1acc[:], ALU.add).then_inc(z1_added, 1)

            def fma(G, gi, s, i, tt, first):
                p, j = s // 5, 2 * (s % 5)
                tile, f = 2 * p + tt, FPB * j + i
                n = FMAS // 2 * p + 8 * (s % 5) + 2 * i + tt
                if i == 0:
                    dve.wait_ge(y_ready, UNITS * G + 4 * s + tt + 1)
                e_col = e_cur[:, f, TPG * gi + tile:TPG * gi + tile + 1]
                y = l2_ps[:, tt, i * M:(i + 1) * M]
                acc = xd[:, gi % 2, tile, :]
                if f == 0:
                    nc.vector.tensor_scalar(acc, y, e_col, None, ALU.mult).then_inc(fma_done, 1)
                else:
                    dve.wait_ge(fma_done, FMAS * G + n - 1)
                    nc.vector.scalar_tensor_tensor(out=acc, in0=y, scalar=e_col, in1=acc, op0=ALU.mult,
                                                   op1=ALU.add).then_inc(fma_done, 1)

            def join_x2(G, par):
                dve.wait_ge(fma_done, FMAS * (G + 1))
                dve.wait_ge(pool_added, ADDS * (G + 1))
                nc.vector.tensor_tensor(xd[:, par], xd[:, par], xp[:, par], ALU.add).then_inc(x2_ready, 1)

            def fold_z1(c, first):
                dve.wait_ge(z1_added, GROUPS * (c + 1))
                if not first:
                    dve.wait_ge(h1_done, c)
                nc.vector.tensor_tensor(z1acc[:, 0:2 * P], z1acc[:, 0:2 * P], z1acc[:, 2 * P:4 * P],
                                        ALU.add).then_inc(z1_fold, 1)
                dve.wait_ge(z1_fold, 2 * c + 1)
                nc.vector.tensor_tensor(z1t[:], z1acc[:, 0:P], z1acc[:, P:2 * P], ALU.add).then_inc(z1_fold, 1)
                dve.wait_ge(z1_fold, 2 * c + 2)

            def relu_h1(c):
                dve.wait_ge(h1_done, c + 1)
                nc.vector.tensor_scalar(h1s[:], l3_ps[:], 0.0, None, ALU.max).then_inc(h1_ready, 1)

            def relu_h2(c):
                dve.wait_ge(h2_done, c + 1)
                nc.vector.tensor_scalar(h2s[:], l3_ps[:, 0:H2], 0.0, None, ALU.max).then_inc(h2_ready, 1)

            def keep_y(c):
                dve.wait_ge(y_done, c + 1)
                nc.vector.tensor_scalar(y_sb[:, bass.ds(c * P, P)], l3_ps[0:1, 0:P], 1.0, None,
                                        ALU.mult).then_inc(y_kept, 1)

            dve.wait_ge(turned_ps, 1)
            form_pairs(0, 0, 0, l2_ps[:, 0, :], 0)
            form_pairs(1, 1, 0, l2_ps[:, 1, :], 0)
            for t in range(KT):
                if t + 2 < KT:
                    form_pairs(t + 2, t + 2, 0, l2_ps[:, (t + 2) % 4, :], t - 1)
                keep_pair_lo(t, t, t % 2, l2_ps[:, t % 4, :])
            keep_x1_lo(0, 0, True)

            def chunk(c, first, last):
                dve.wait_ge(gathered, 16 * F * (c + 1))
                if not first:
                    dve.wait_ge(fma_done, FMAS * GROUPS * c)
                nc.vector.tensor_copy(e_cur[:], e_next[:]).then_inc(e_cur_ok, 1)
                dve.wait_ge(e_cur_ok, c + 1)
                for gi in range(GROUPS):
                    G = 4 * c + gi
                    ahead = not (last and gi == GROUPS - 1)
                    if not (first and gi < 2):
                        dve.wait_ge(x2_stored, 16 * (G - 1))
                    for s in range(SLOTS):
                        for i in range(FPB):
                            for tt in range(2):
                                fma(G, gi, s, i, tt, first)
                        if ahead and 1 <= s <= KT:
                            keep_pair_lo(KT * (G + 1) + s - 1, s - 1, (KT * (gi + 1) + s - 1) % 2, pair_ps)
                        if ahead and s < KT:
                            form_pairs(KT * (G + 1) + s, s, G + 1, pair_ps, KT * (G + 1) + s)
                        if ahead and s == KT + 1:
                            keep_x1_lo(G + 1, (gi + 1) % GROUPS, first)
                        if s == 3 and not (first and gi == 0):
                            join_x2(G - 1, (gi - 1) % 2)
                        if gi == 3 and s == 5:
                            if not first:
                                relu_h1(c - 1)
                            fold_z1(c, first)
                        if gi == 3 and s == 8 and not first:
                            relu_h2(c - 1)
                if not first:
                    keep_y(c - 1)

            chunk(0, True, False)
            with dve.Fori(1, CHUNKS - 1) as c:
                chunk(c, False, False)
            chunk(CHUNKS - 1, False, True)
            end = CHUNKS - 1
            join_x2(4 * end + 3, 1)
            relu_h1(end)
            relu_h2(end)
            keep_y(end)

        @block.tensor
        def _(pe):
            def turn(G):
                pe.wait_ge(tripled_ok, G + 1)
                if not (isinstance(G, int) and G == 0):
                    pe.wait_ge(pairs_ok, KT * G)
                for k in range(TPG):
                    last = nc.tensor.transpose(turn_ps[0:KPT * F, k * P:(k + 1) * P],
                                               tripled[:, k].rearrange("p k f -> p (k f)"), ident[:])
                last.then_inc(turned_ps, 1)

            def contract_pairs(n, t, slot):
                pe.wait_ge(pair_lo, n + 1)
                r = ROWS[t]
                w = slice(t * M, (t + 1) * M)
                nc.tensor.matmul(l1_ps[:], w0h[0:r, w], ph[0:r, slot, :], start=(t == 0), stop=False)
                nc.tensor.matmul(l1_ps[:], w0h[0:r, w], pl[0:r, slot, :], start=False, stop=False)
                nc.tensor.matmul(l1_ps[:], w0l[0:r, w], ph[0:r, slot, :], start=False,
                                 stop=(t == KT - 1)).then_inc(l1_done, 1)

            def layer2(G, gi, u, first):
                p, j, tt = u // 20, (u % 20) // 2, u % 2
                if not (first and gi == 0 and u < 4):
                    if j % 2 == 0:
                        pe.wait_ge(fma_done, FMAS * G + FMAS // 2 * p + 4 * j - 1 + tt)
                    else:
                        pe.wait_ge(act_scaled, SCALED * G + 10 * p + j - 2 + tt)
                cols = slice((2 * p + tt) * P, (2 * p + tt + 1) * P)
                rows = slice(FPB * j * M, (FPB * j + NF[j]) * M)
                y = l2_ps[:, u % 4, 0:NF[j] * M]
                xh, xl = x1h[:, gi % 2, cols], x1l[:, gi % 2, cols]
                nc.tensor.matmul(y, xh, w1h[:, rows], start=True, stop=False)
                nc.tensor.matmul(y, xh, w1l[:, rows], start=False, stop=False)
                nc.tensor.matmul(y, xl, w1h[:, rows], start=False, stop=True).then_inc(y_ready, 1)

            def layer3_g(c, q, bank, free=True):
                if q == 0:
                    pe.wait_ge(x2q_in, 16 * SB8 * (c + 1))
                    pe.wait_ge(eblk_in, 16 * SB8 * (c + 1))
                elif free:
                    pe.wait_ge(g_kept, QS * c + q)
                nc.tensor.matmul(bank[:, 0:SB8 * FG], x2q[:, q, :], eblk[:, q, :], start=True,
                                 stop=True).then_inc(g_done, 1)

            def layer3_f(c, f):
                if f == 0:
                    pe.wait_ge(g_kept, QS * (c + 1))
                mm = nc.tensor.matmul(l3_ps[:, 0:P], w2[:, f, :], gs[:, f, :], start=(f == 0), stop=(f == F - 1))
                if f == F - 1:
                    mm.then_inc(z3_done, 1)

            def mlp1(c, m):
                if m == 0:
                    pe.wait_ge(z3_ready, c + 1)
                    pe.wait_ge(z1_fold, 2 * (c + 1))
                cols = slice(m * P, (m + 1) * P)
                for k, z in enumerate((z1t[:], gs[:, F, :], z3t[:])):
                    nc.tensor.matmul(l3_ps[:, cols], wt1[:, k, cols], z, start=(k == 0), stop=False)
                mm = nc.tensor.matmul(l3_ps[:, cols], wtd[:, cols], dense_sb[:, bass.ds(c * P, P)], start=False, stop=True)
                if m == H1 // P - 1:
                    mm.then_inc(h1_done, 1)

            def mlp2(c, m):
                if m == 0:
                    pe.wait_ge(h1_ready, c + 1)
                cols = slice(m * P, (m + 1) * P)
                for k in range(H1 // P):
                    nc.tensor.matmul(l3_ps[:, cols], wt2[:, k, cols], h1s[:, k * P:(k + 1) * P],
                                     start=(k == 0), stop=False)
                mm = nc.tensor.matmul(l3_ps[:, cols], bt2[:, cols], ones_row[:], start=False, stop=True)
                if m == H2 // P - 1:
                    mm.then_inc(h2_done, 1)

            def mlp3(c):
                pe.wait_ge(h2_ready, c + 1)
                for k in range(H2 // P):
                    mm = nc.tensor.matmul(l3_ps[0:1, 0:P], wt3[:, k:k + 1], h2s[:, k * P:(k + 1) * P],
                                          start=(k == 0), stop=(k == H2 // P - 1))
                mm.then_inc(y_done, 1)

            pe.wait_ge(ident_ok, 1)
            pe.wait_ge(w0h_ok, 1)
            pe.wait_ge(w0l_ok, 1)
            turn(0)
            for t in range(KT):
                contract_pairs(t, t, t % 2)
            pe.wait_ge(w1l_ok, 1)
            pe.wait_ge(w2_in, 16)
            pe.wait_ge(top_in, 96)
            pe.wait_ge(filled, 4)
            pe.wait_ge(dense_in, 16)

            def layer3_and_mlp(c, gi, s, v):
                q = 2 * (SLOTS * gi + s - G_SLOT) + v // 2
                if v % 2 and 0 <= q < QS:
                    layer3_g(c, q, l3_ps)
                f = 3 * (SLOTS * gi + s - F_SLOT) + (0, 1, 0, 2)[v]
                if v != 2 and 0 <= f < F:
                    layer3_f(c, f)
                if gi == 3 and v == 3 and s < H1 // P:
                    mlp1(c, s)
                if gi == 3 and v == 3 and 6 <= s < 6 + H2 // P:
                    mlp2(c, s - 6)

            def chunk(c, first, last):
                for gi in range(GROUPS):
                    G = 4 * c + gi
                    ahead = not (last and gi == GROUPS - 1)
                    pe.wait_ge(x1_lo, G + 1)
                    for s in range(SLOTS):
                        if ahead and s == 0:
                            turn(G + 1)
                        for v in range(4):
                            layer2(G, gi, 4 * s + v, first)
                            if v == 1 and ahead and 2 <= s < 2 + KT:
                                t = s - 2
                                if t == 0:
                                    pe.wait_ge(z1_added, G + 1)
                                contract_pairs(KT * (G + 1) + t, t, (KT * (gi + 1) + t) % 2)
                            if not first:
                                layer3_and_mlp(c - 1, gi, s, v)
                if not first:
                    mlp3(c - 1)

            chunk(0, True, False)
            with pe.Fori(1, CHUNKS - 1) as c:
                chunk(c, False, False)
            chunk(CHUNKS - 1, False, True)
            end = CHUNKS - 1
            for q in range(QS):
                if q >= 4:
                    pe.wait_ge(g_kept, QS * end + q - 3)
                layer3_g(end, q, l2_ps[:, q % 4, :], False)
            for f in range(F):
                layer3_f(end, f)
            for m in range(H1 // P):
                mlp1(end, m)
            for m in range(H2 // P):
                mlp2(end, m)
            mlp3(end)


def kernel(**inputs):
    import concourse.bacc as _bacc
    from concourse.bass_utils import run_bass_kernel_spmd as _run

    f0 = np.asarray(inputs["L0_rec_f0"])
    a, b = pair_rows()
    w0 = np.zeros((2, KT * KPT * F, M), f0.dtype)
    w0[0, :a.size] = f0[a]
    w0[1, F:b.size] = f0[b[F:]]
    w0 = np.ascontiguousarray(w0.reshape(2, KT, KPT * F, M).transpose(0, 2, 1, 3)).reshape(2, KPT * F, KT * M)
    arrays = {"ids": np.ascontiguousarray(inputs["ids"])}
    for f in range(F):
        arrays[f"tbl_{f}"] = np.ascontiguousarray(inputs[f"tbl_{f}"])
    arrays["w0a"], arrays["w0b"] = np.ascontiguousarray(w0[0]), np.ascontiguousarray(w0[1])
    for name, key in (("f1", "L0_rec_f1"), ("f2", "L0_rec_f2"), ("wt1", "W_top1"), ("wt2", "W_top2")):
        arrays[name] = np.ascontiguousarray(inputs[key])
    arrays["wt3"] = np.ascontiguousarray(np.asarray(inputs["W_top3"]).reshape(H2 // P, P).T)
    arrays["bt1"] = np.ascontiguousarray(inputs["b_top1"]).reshape(1, H1)
    arrays["bt2"] = np.ascontiguousarray(inputs["b_top2"]).reshape(1, H2)
    arrays["dense_t"] = np.ascontiguousarray(np.asarray(inputs["dense_ctx"]).T)

    nc = _bacc.Bacc("TRN2", target_bir_lowering=False, num_devices=1)
    ap = {k: nc.dram_tensor(f"in_{k}", v.shape, mybir.dt.from_np(v.dtype), kind="ExternalInput").ap()
          for k, v in arrays.items()}
    out = nc.dram_tensor("out_y", (1, B), F32, kind="ExternalOutput").ap()
    build(nc, ap["ids"], [ap[f"tbl_{f}"] for f in range(F)], ap["w0a"], ap["w0b"], ap["f1"], ap["f2"],
          ap["wt1"], ap["bt1"], ap["wt2"], ap["bt2"], ap["wt3"], ap["dense_t"], out)
    r = _run(nc, [{f"in_{k}": v for k, v in arrays.items()}], core_ids=[0])
    return r.results[0]["out_y"].reshape(B, 1)
```

```python
from contextlib import ExitStack

import numpy as np
import concourse.bass as bass
from concourse import mybir

F32 = mybir.dt.float32
F32R = mybir.dt.float32r
I32 = mybir.dt.int32
ALU = mybir.AluOpType
ACT = mybir.ActivationFunctionType

P = 128
B, F, D, M = 512, 39, 16, 128
CHUNKS = B // P
TPG = 4
GROUPS = D // TPG
COLS = TPG * P
NK = F // 2 + 1
KPT = P // F
KT = -(-NK // KPT)
ROWS = [F * min(KPT, NK - KPT * t) for t in range(KT)]
FPB = 4
BLOCKS = -(-F // FPB)
NF = [FPB] * BLOCKS
NF[4] -= FPB * BLOCKS - F
FOFF = [sum(NF[:j]) for j in range(BLOCKS)]
VOFF = [sum(NF[0:j:2]) for j in range(0, BLOCKS + 1, 2)]
PAIRS = TPG // 2
UNITS = TPG * BLOCKS
FMAS = TPG * VOFF[-1]
SKEWED = (0, 1, 8, 9)
SCALED = TPG * BLOCKS // 2
ADDS = PAIRS * 2 * (BLOCKS // 2 + 1)
SLOTS = BLOCKS
SB8 = P // D
QS = P // SB8
FG = F + 1
H1, H2 = 512, 256
ZT = 3
DENSE = 16
GATHERS = [[2, 1, 1, 1, 1, 2]] * 4 + [[2, 2, 1, 1, 1, 0]] + [[0] * 6] * 3
EARLY = 21
FIRST_GATHERS = [[1, 1, 1, 0, 1, 0]] * 5 + [[0] * 6] * 3
W0_AFTER = 3
W1_CUT = 20 * M
DIRECT = 2
SMALL_K = {1000: 8, 1250: 16}
TURN_SLOT = 8
G_SLOT, F_SLOT = 6, 14


def pair_rows():
    k = np.arange(NK)[:, None]
    f = np.arange(F)[None, :]
    g = (f + k) % F
    return (f * F + g).reshape(-1), (g * F + f).reshape(-1)


def fma_order(s):
    n = NF[2 * (s % 5)]
    if s in SKEWED:
        return [(0, 0)] + [x for i in range(n - 1) for x in ((i + 1, 0), (i, 1))] + [(n - 1, 1)]
    return [(i, tt) for i in range(n) for tt in range(2)]


def fma_count(s, i, tt):
    return FMAS // 2 * (s // 5) + 2 * VOFF[s % 5] + fma_order(s).index((i, tt)) + 1


def lookup_plan(rows):
    per_k = {k: [f for f, n in enumerate(rows) if SMALL_K.get(n) == k] for k in SMALL_K.values()}
    batches = []
    for k, fs in per_k.items():
        n = COLS // (k * D)
        batches += [(k, i, fs[i:i + n]) for i in range(0, len(fs), n)]
    return per_k, batches


def build(nc, ids, tables, w0a_d, w0b_d, f1, f2, wt1_d, bt1_d, wt2_d, bt2_d, wt3_d, dense_t, rank_d, small_d, small_ids,
          out):
    per_k, batches = lookup_plan([t.shape[0] for t in tables])
    small = sum(per_k.values(), [])
    others = [f for f in range(F) if f not in small]

    def gathers(c):
        return 16 * F * c + 16 * len(others)

    ctx = ExitStack()
    with ctx:
        def sb(name, shape, dt=F32):
            return ctx.enter_context(nc.sbuf_tensor(name, shape, dt))

        def sem(name):
            return ctx.enter_context(nc.semaphore(name))

        w1h = sb("w1h", [P, F * M], F32R)
        w1l = sb("w1l", [P, F * M], F32R)
        w0h = sb("w0h", [P, KT * M], F32R)
        w0l = sb("w0l", [P, KT * M], F32R)
        w2 = sb("w2", [P, F, M])
        wt1 = sb("wt1", [P, ZT, H1])
        wtd = sb("wtd", [DENSE + 1, H1])
        wt2 = sb("wt2", [P, H1 // P, H2])
        bt2 = sb("bt2", [1, H2])
        wt3 = sb("wt3", [P, H2 // P])
        ident = sb("ident", [P, P])
        ones_row = sb("ones_row", [1, P])
        idx_all = sb("idx_all", [P, CHUNKS, F], I32)
        idx_cur = sb("idx_cur", [P, F], I32)
        e_next = sb("e_next", [P, F, D])
        e_cur = sb("e_cur", [P, F, D])
        ep = sb("ep", [P, D, FG])
        tripled = sb("tripled", [P, TPG, KPT, F])
        turned = sb("turned", [KPT * F, COLS])
        shifted = sb("shifted", [KPT * F, KT, COLS])
        ph = sb("ph", [P, 2, COLS], F32R)
        pl = sb("pl", [P, 2, COLS], F32R)
        x1h = sb("x1h", [P, 2, COLS], F32R)
        x1l = sb("x1l", [P, 2, COLS], F32R)
        scaled = sb("scaled", [P, BLOCKS, FPB * M])
        xd = sb("xd", [P, 2, TPG, M])
        xp = sb("xp", [P, 2, TPG, M])
        z1acc = sb("z1acc", [P, COLS])
        z1t = sb("z1t", [P, P])
        x2q = sb("x2q", [P, QS, M])
        eblk = sb("eblk", [P, QS, SB8 * FG])
        gs = sb("gs", [P, FG, P])
        z3t = sb("z3t", [P, P])
        dense_sb = sb("dense_sb", [DENSE + 1, B])
        h1s = sb("h1s", [P, H1])
        h2s = sb("h2s", [P, H2])
        y_sb = sb("y_sb", [1, B])

        w1_raw = gs[:].rearrange("p f b -> p (f b)")[:, 0:F * M]
        raw = scaled[:].rearrange("p s n -> p (s n)")
        w0_a, w0_b, w0_s = (raw[0:ROWS[0], n * KT * M:(n + 1) * KT * M] for n in range(3))

        spare = {8: x2q[:].rearrange("p q m -> p (q m)"), 16: shifted[:].rearrange("p t n -> p (t n)")}
        small_tables = {k: spare[k][0:small_d[k].shape[0], 0:small_d[k].shape[1]] for k in per_k}
        one_hots = [xd[:, n].rearrange("p t m -> p (t m)") for n in range(2)]
        chosen = xp[:, 0].rearrange("p t m -> p (t m)")
        looked = xp[:, 1].rearrange("p t m -> p (t m)")
        cut = {k: [h1s[:, (4 * n + i) * F:(4 * n + i) * F + len(fs)] for i in range(4)]
               for n, (k, fs) in enumerate(per_k.items())}
        idx_small = {k: h1s[:, (8 + n) * F:(8 + n) * F + len(fs)].bitcast(I32) for n, (k, fs) in enumerate(per_k.items())}
        widest = max(per_k)
        rank = z1acc[:, 0:widest + 1]
        mask = z1acc[:, widest + 1:widest + 1 + sum(k * len(fs) for k, fs in per_k.items())]
        mask_at = {f: sum(k2 * len(fs2) for k2, fs2 in per_k.items() if k2 < k) + k * i
                   for k, fs in per_k.items() for i, f in enumerate(fs)}

        l2_ps = ctx.enter_context(nc.psum_tensor("l2_ps", [P, 4, 512], F32))
        turn_ps = ctx.enter_context(nc.psum_tensor("turn_ps", [P, 512], F32))
        pair_ps = ctx.enter_context(nc.psum_tensor("pair_ps", [P, 512], F32))
        l1_ps = ctx.enter_context(nc.psum_tensor("l1_ps", [P, 512], F32))
        l3_ps = ctx.enter_context(nc.psum_tensor("l3_ps", [P, 512], F32))

        x2_dram = nc.dram_tensor("x2_dram", [P, D, M], F32, kind="Internal").ap()
        turned_dram = nc.dram_tensor("turned_dram", [F + NK - 1, COLS], F32, kind="Internal").ap()
        e_dram = nc.dram_tensor("e_dram", [P, D, FG], F32, kind="Internal").ap()

        small_ids_in = sem("small_ids_in")
        rank_in, tables_in, cut_ok, cut_f32_ok = (sem(n) for n in ("rank_in", "tables_in", "cut_ok", "cut_f32_ok"))
        mask_ok = sem("mask_ok")
        spread = sem("spread")
        one_hot = sem("one_hot")
        looked_up = sem("looked_up")
        masked = sem("masked")
        picked = sem("picked")
        looked_kept = sem("looked_kept")
        ids_in, w0_in, w1_in, w2_in, top_in = (sem(n) for n in ("ids_in", "w0_in", "w1_in", "w2_in", "top_in"))
        w0_sum, w0h_ok, w0l_ok, w1h_ok, w1l_ok = (sem(n) for n in ("w0_sum", "w0h_ok", "w0l_ok", "w1h_ok", "w1l_ok"))
        ident_zero, ident_ok, filled = sem("ident_zero"), sem("ident_ok"), sem("filled")
        eblk_zero = sem("eblk_zero")
        idx_ok, gathered, e_cur_ok = sem("idx_ok"), sem("gathered"), sem("e_cur_ok")
        tripled_ok = sem("tripled_ok")
        turned_ps = sem("turned_ps")
        turned_stored = sem("turned_stored")
        turned_ok = sem("turned_ok")
        shifted_in = [sem(f"shifted_in{t}") for t in range(KT)]
        pairs_ok = sem("pairs_ok")
        pair_hi = sem("pair_hi")
        pair_lo = sem("pair_lo")
        l1_done = sem("l1_done")
        x1_hi, x1_lo, z1_added = sem("x1_hi"), sem("x1_lo"), sem("z1_added")
        y_ready = sem("y_ready")
        fma_done = sem("fma_done")
        act_scaled = sem("act_scaled")
        last_added = sem("last_added")
        pool_added = sem("pool_added")
        x2_ready, x2_stored, x2q_in = sem("x2_ready"), sem("x2_stored"), sem("x2q_in")
        ep_ready, ep_stored, eblk_in = sem("ep_ready"), sem("ep_stored"), sem("eblk_in")
        g_done, g_kept, z3_done, z3_ready = sem("g_done"), sem("g_kept"), sem("z3_done"), sem("z3_ready")
        z1_fold, dense_in = sem("z1_fold"), sem("dense_in")
        h1_done, h1_ready, h2_done, h2_ready = sem("h1_done"), sem("h1_ready"), sem("h2_done"), sem("h2_ready")
        y_done, y_kept, y_out = sem("y_done"), sem("y_kept"), sem("y_out")

        block = ctx.enter_context(nc.Block())

        @block.sync
        def _(sp):
            sp.dma_start(idx_all[:], ids.rearrange("(c p) f -> p c f", p=P)).then_inc(ids_in, 16)
            sp.dma_start(rank, rank_d).then_inc(rank_in, 16)
            for k in per_k:
                sp.dma_start(idx_small[k], small_ids[k]).then_inc(small_ids_in, 16)
            for k in per_k:
                sp.dma_start(small_tables[k], small_d[k]).then_inc(tables_in, 16)
            sp.dma_start(w0_a, w0a_d).then_inc(w0_in, 16)
            sp.dma_start(w0_b, w0b_d).then_inc(w0_in, 16)
            sp.dma_start(w1_raw.rearrange("p (f m) -> p f m", m=M),
                         f1.rearrange("(f g) m -> g f m", g=M)).then_inc(w1_in, 16)
            sp.wait_ge(filled, 3)
            sp.dma_start(dense_sb[0:DENSE, :], dense_t).then_inc(dense_in, 16)

            def shift(G):
                sp.wait_ge(turned_ok, G + 1)
                for t in range(KT):
                    sp.wait_ge(pairs_ok, KT * (G - 1) + t + 1)
                    if isinstance(G, int) and G == 1:
                        sp.wait_ge(l1_done, t + 1)
                    for j in range(ROWS[t] // F):
                        k = KPT * t + j
                        sp.dma_start(shifted[j * F:(j + 1) * F, t, :],
                                     turned[k:k + F, :]).then_inc(shifted_in[t], 16)

            def store_x2(c, gi):
                sp.wait_ge(x2_ready, 4 * c + gi + 1)
                sp.dma_start(x2_dram[:, TPG * gi:TPG * gi + TPG, :],
                             xd[:, gi % 2]).then_inc(x2_stored, 16)

            def load_x2q(d0, n):
                for d in range(d0, d0 + n):
                    sp.dma_start(x2q[d * SB8:(d + 1) * SB8, :, :],
                                 x2_dram.rearrange("(q s) d m -> d s q m", s=SB8)[d]).then_inc(x2q_in, 16)

            def chunk(c, first, last):
                for gi in range(GROUPS):
                    if gi == 0 and not first:
                        store_x2(c - 1, 3)
                        sp.wait_ge(x2_stored, 64 * c)
                        load_x2q(TPG * 3, TPG)
                        sp.wait_ge(eblk_in, 16 * SB8 * c)
                    if gi == 1:
                        if not first:
                            sp.wait_ge(x2q_in, 16 * D * c)
                        store_x2(c, 0)
                        sp.wait_ge(ep_ready, c + 1)
                        sp.dma_start(e_dram, ep[:]).then_inc(ep_stored, 16)
                    if gi == 2:
                        store_x2(c, 1)
                        sp.wait_ge(x2_stored, 64 * c + 32)
                        if not first:
                            sp.wait_ge(z3_done, c)
                        load_x2q(0, 2 * TPG)
                        sp.wait_ge(ep_stored, 16 * c + 16)
                        if first:
                            sp.wait_ge(eblk_zero, 1)
                        for s in range(SB8):
                            sp.dma_start(eblk[s:P:SB8, :, s * FG:(s + 1) * FG],
                                         e_dram.rearrange("(q s) d f -> s d q f", s=SB8)[s]).then_inc(eblk_in, 16)
                    if gi == 3:
                        store_x2(c, 2)
                        sp.wait_ge(x2_stored, 64 * c + 48)
                        load_x2q(2 * TPG, TPG)
                    if not (last and gi >= GROUPS - 2):
                        shift(4 * c + gi + 2)

            sp.wait_ge(turned_ok, 1)
            for t in range(DIRECT):
                for j in range(KPT):
                    k = KPT * t + j
                    sp.dma_start(shifted[j * F:(j + 1) * F, t, :], turned[k:k + F, :]).then_inc(shifted_in[t], 16)
                if t == 0:
                    sp.dma_start(turned_dram, turned[0:F + NK - 1, :]).then_inc(turned_stored, 16)
            sp.wait_ge(turned_stored, 16)
            for t in range(DIRECT, KT):
                rows = turned_dram[KPT * t:KPT * t + F, :]
                overlapping = bass.AP(tensor=rows.tensor, offset=rows.offset,
                                      ap=[[COLS, ROWS[t] // F], [COLS, F], [1, COLS]])
                sp.dma_start(shifted[0:ROWS[t], t, :], overlapping).then_inc(shifted_in[t], 16)

            shift(1)
            sp.dma_start(w2[:], f2.rearrange("(f g) m -> g f m", g=M)).then_inc(w2_in, 16)
            sp.dma_start(wt1[:], wt1_d[0:ZT * P, :].rearrange("(k p) n -> p k n", p=P)).then_inc(top_in, 16)
            sp.dma_start(wtd[0:DENSE, :], wt1_d[ZT * P:ZT * P + DENSE, :]).then_inc(top_in, 16)
            sp.dma_start(wtd[DENSE:DENSE + 1, :], bt1_d).then_inc(top_in, 16)
            sp.dma_start(wt2[:], wt2_d.rearrange("(k p) n -> p k n", p=P)).then_inc(top_in, 16)
            sp.dma_start(bt2[:], bt2_d).then_inc(top_in, 16)
            sp.dma_start(wt3[:], wt3_d).then_inc(top_in, 16)
            chunk(0, True, False)
            with sp.Fori(1, CHUNKS - 1) as c:
                chunk(c, False, False)
            chunk(CHUNKS - 1, False, True)
            for p in range(PAIRS):
                d = D - TPG + 2 * p
                sp.wait_ge(x2_ready, CHUNKS * GROUPS + p)
                sp.dma_start(x2_dram[:, d:d + 2, :], xd[:, 1, 2 * p:2 * p + 2]).then_inc(x2_stored, 16)
                sp.wait_ge(x2_stored, 16 * (CHUNKS * GROUPS + p))
                load_x2q(d, 2)
            sp.wait_ge(y_kept, CHUNKS)
            sp.dma_start(out, y_sb[:]).then_inc(y_out, 16)
            sp.wait_ge(y_out, 16)

        @block.gpsimd
        def _(pool):
            nc.gpsimd.memset(ident[:], 0.0).then_inc(ident_zero, 1)
            pool.wait_ge(ident_zero, 1)
            nc.gpsimd.affine_select(out=ident[:], in_=ident[:], compare_op=ALU.not_equal, fill=1.0, base=0,
                                    pattern=[[-1, P]], channel_multiplier=1).then_inc(ident_ok, 1)

            def gather(f):
                nc.gpsimd.indirect_dma_start(
                    out=e_next[:, f, :], out_offset=None, in_=tables[f],
                    in_offset=bass.IndirectOffsetOnAxis(ap=idx_cur[:, f:f + 1], axis=0)).then_inc(gathered, 16)

            pool.wait_ge(ids_in, 16)
            nc.gpsimd.tensor_copy(idx_cur[:], idx_all[:, 0, :]).then_inc(idx_ok, 1)
            pool.wait_ge(idx_ok, 1)
            for f in others:
                gather(f)

            pool.wait_ge(w1h_ok, 2)
            nc.gpsimd.tensor_tensor(w1l[:, W1_CUT:], w1_raw[:, W1_CUT:], w1h[:, W1_CUT:].bitcast(F32),
                                    ALU.subtract).then_inc(w1l_ok, 1)

            def add(G, gi, p, step, tt, alone=False):
                n = 12 * p + 2 * step + tt
                if alone:
                    n = 12 * p + 6 + step - 3 + 1
                if step < 4:
                    pool.wait_ge(act_scaled, SCALED * G + 10 * p + 2 * (step + 1) + tt + 1)
                if step > 0:
                    pool.wait_ge(pool_added, ADDS * G + n - 1)
                s = [scaled[:, 2 * ja + tt, :] for ja in range(5)]
                if step < 3:
                    nc.gpsimd.tensor_tensor(s[step + 1], s[step], s[step + 1], ALU.add).then_inc(pool_added, 1)
                elif step == 3:
                    nc.gpsimd.tensor_tensor(s[3], s[3], s[4], ALU.add).then_inc(pool_added, 1)
                elif step == 4:
                    nc.gpsimd.tensor_tensor(s[3][:, 0:2 * M], s[3][:, 0:2 * M], s[3][:, 2 * M:4 * M],
                                            ALU.add).then_inc(pool_added, 1)
                else:
                    nc.gpsimd.tensor_tensor(xp[:, gi % 2, 2 * p + tt, :], s[3][:, 0:M], s[3][:, M:2 * M],
                                            ALU.add).then_inc(pool_added, 1)

            def take_indices(c, first):
                pool.wait_ge(gathered, gathers(c))
                nc.gpsimd.tensor_copy(idx_cur[:], idx_all[:].rearrange("p c f -> p (c f)")
                                      [:, bass.ds((c + 1) * F, F)]).then_inc(idx_ok, 1)
                pool.wait_ge(idx_ok, c + 2)
                pool.wait_ge(e_cur_ok, c + 1)
                pool.wait_ge(ep_ready, c + 1)
                pool.wait_ge(tripled_ok, GROUPS * c + (1 if first else 2))

            def chunk(c, first, last):
                todo = [] if last else list(range(F))
                plan = FIRST_GATHERS if first else GATHERS
                if first:
                    take_indices(c, True)
                    for f in todo[:EARLY]:
                        gather(f)
                    del todo[:EARLY]
                for gi in range(GROUPS):
                    G = 4 * c + gi
                    for p in range(PAIRS):
                        for step in range(6):
                            if step == 5 and p == 0 and not (first and gi < 2):
                                pool.wait_ge(x2_ready, G - 1)
                            add(G, gi, p, step, 0, last and gi == GROUPS - 1 and p == 1 and step > 3)
                            if not (first or last) and gi == p == step == 0:
                                take_indices(c, False)
                            if not (last and gi == GROUPS - 1 and p == 1 and step >= 3):
                                add(G, gi, p, step, 1)
                            n = plan[PAIRS * gi + p][step]
                            for f in todo[:n]:
                                gather(f)
                            del todo[:n]

            chunk(0, True, False)
            with pool.Fori(1, CHUNKS - 1) as c:
                chunk(c, False, False)
            chunk(CHUNKS - 1, False, True)

        @block.scalar
        def _(act):
            act.wait_ge(w1_in, 16)
            nc.scalar.copy(w1h[:, 0:W1_CUT], w1_raw[:, 0:W1_CUT]).then_inc(w1h_ok, 1)
            act.wait_ge(w0_sum, 1)
            nc.scalar.copy(w0h[0:ROWS[0], :], w0_s).then_inc(w0h_ok, 1)
            nc.scalar.copy(w1h[:, W1_CUT:], w1_raw[:, W1_CUT:]).then_inc(w1h_ok, 1)

            def triple(G, gi, e):
                if not (isinstance(G, int) and G == 0):
                    act.wait_ge(turned_ps, G)
                base = e[:, TPG * gi:TPG * gi + TPG, 0:F]
                rep = bass.AP(tensor=base.tensor, offset=base.offset,
                              ap=[list(base.ap[0]), list(base.ap[1]), [0, KPT], list(base.ap[2])])
                nc.scalar.copy(tripled[:], rep).then_inc(tripled_ok, 1)

            def keep_turned(G):
                act.wait_ge(turned_ps, G + 1)
                if not (isinstance(G, int) and G == 0):
                    act.wait_ge(pairs_ok, KT * G)
                nc.scalar.copy(turned[:], turn_ps[0:KPT * F, :]).then_inc(turned_ok, 1)

            def keep_pair_hi(n, t, slot, bank):
                act.wait_ge(pairs_ok, n + 1)
                act.wait_ge(l1_done, n - 1)
                r = ROWS[t]
                nc.scalar.copy(ph[0:r, slot, :], bank[0:r, :]).then_inc(pair_hi, 1)

            def keep_x1_hi(G, par, early):
                act.wait_ge(l1_done, KT * (G + 1))
                if not early:
                    act.wait_ge(y_ready, UNITS * (G - 1))
                nc.scalar.copy(x1h[:, par, :], l1_ps[:]).then_inc(x1_hi, 1)

            def scale(G, gi, s, tt, first):
                p, j = s // 5, 2 * (s % 5) + 1
                tile, ja = 2 * p + tt, j // 2
                act.wait_ge(y_ready, UNITS * G + 4 * s + 2 + tt + 1)
                if not (first and gi == 0 and p == 0):
                    free = (0, 1, 2, 5, 3)[ja]
                    act.wait_ge(pool_added, ADDS * G + 12 * (p - 1) + 2 * free + tt + 1)
                for i in range(NF[j]):
                    last = nc.scalar.activation(scaled[:, 2 * ja + tt, i * M:(i + 1) * M],
                                                l2_ps[:, 2 + tt, i * M:(i + 1) * M], ACT.Copy,
                                                scale=ep[:, TPG * gi + tile, FOFF[j] + i:FOFF[j] + i + 1])
                last.then_inc(act_scaled, 1)

            def keep_g(c, q, bank):
                act.wait_ge(g_done, QS * c + q + 1)
                nc.scalar.copy(gs[:].rearrange("p f b -> p b f")[:, SB8 * q:SB8 * (q + 1), :],
                               bank[:, 0:SB8 * FG].rearrange("p (b f) -> p b f", f=FG)).then_inc(g_kept, 1)

            def keep_z3(c):
                act.wait_ge(z3_done, c + 1)
                nc.scalar.copy(z3t[:], l3_ps[:, 0:P]).then_inc(z3_ready, 1)

            def keep_ep(c):
                nc.scalar.copy(ep[:, :, 0:F], e_turned).then_inc(ep_ready, 1)
                act.wait_ge(ep_ready, c + 1)

            for b, (_, _, fs) in enumerate(batches):
                act.wait_ge(picked, b + 1)
                for f in fs:
                    n = small.index(f)
                    nc.scalar.copy(e_next[:, f, :], looked[:, n * D:(n + 1) * D]).then_inc(looked_kept, 1)

            e_turned = e_next[:].rearrange("p f d -> p d f")

            act.wait_ge(gathered, gathers(0))
            act.wait_ge(looked_kept, len(small))
            triple(0, 0, e_turned)
            keep_turned(0)
            act.wait_ge(filled, 3)
            keep_ep(0)
            triple(1, 1, ep)
            act.wait_ge(rank_in, 16)
            zero = rank[:, 0:1]
            zeros = bass.AP(tensor=zero.tensor, offset=zero.offset, ap=[list(zero.ap[0]), [0, QS * SB8 * FG]])
            nc.scalar.copy(eblk[:].rearrange("p q n -> p (q n)"), zeros).then_inc(eblk_zero, 1)
            keep_x1_hi(0, 0, True)
            keep_turned(1)

            def chunk(c, first, last):
                if not first:
                    act.wait_ge(act_scaled, SCALED * GROUPS * c)
                    act.wait_ge(ep_stored, 16 * c)
                    keep_ep(c)
                for gi in range(GROUPS):
                    G = 4 * c + gi
                    ahead = not (last and gi == GROUPS - 1)
                    two_ahead = not (last and gi >= GROUPS - 2)
                    for s in range(SLOTS):
                        if two_ahead and s == SLOTS - 1:
                            keep_turned(G + 2)
                        if ahead and 1 <= s <= KT:
                            keep_pair_hi(KT * (G + 1) + s - 1, s - 1, (KT * (gi + 1) + s - 1) % 2, pair_ps)
                        if ahead and s == KT + 1:
                            keep_x1_hi(G + 1, (gi + 1) % 2, first and gi == 0)
                        q = 2 * (SLOTS * gi + s - G_SLOT)
                        if not first and 0 <= q < QS:
                            keep_g(c - 1, q, l3_ps)
                        scale(G, gi, s, 0, first)
                        scale(G, gi, s, 1, first)
                        if not first and 0 <= q < QS:
                            keep_g(c - 1, q + 1, l3_ps)
                        if gi == 2 and not first and s == SLOTS - 1:
                            keep_z3(c - 1)
                        if s == TURN_SLOT - 1 and gi < 2:
                            triple(G + 2, gi + 2, ep)
                        if s == TURN_SLOT - 1 and gi >= 2 and two_ahead:
                            act.wait_ge(gathered, gathers(c + 1))
                            triple(G + 2, gi - 2, e_turned)

            chunk(0, True, False)
            with act.Fori(1, CHUNKS - 1) as c:
                chunk(c, False, False)
            chunk(CHUNKS - 1, False, True)
            for q in range(QS):
                keep_g(CHUNKS - 1, q, l2_ps[:, q % 4, :])
            keep_z3(CHUNKS - 1)

        @block.vector
        def _(dve):
            nc.vector.memset(ones_row[:], 1.0).then_inc(filled, 1)
            nc.vector.memset(dense_sb[:], 1.0).then_inc(filled, 1)
            nc.vector.memset(ep[:], 1.0).then_inc(filled, 1)
            dve.wait_ge(small_ids_in, 16 * len(per_k))
            for k in per_k:
                nc.vector.tensor_scalar(cut[k][0].bitcast(I32), idx_small[k], k.bit_length() - 1, None,
                                        ALU.arith_shift_right).then_inc(cut_ok, 1)
                nc.vector.tensor_scalar(cut[k][1].bitcast(I32), idx_small[k], k - 1, None,
                                        ALU.bitwise_and).then_inc(cut_ok, 1)
            for n, k in enumerate(per_k):
                dve.wait_ge(cut_ok, 2 * n + 2)
                nc.vector.tensor_copy(cut[k][2], cut[k][0].bitcast(I32)).then_inc(cut_f32_ok, 1)
                nc.vector.tensor_copy(cut[k][3], cut[k][1].bitcast(I32)).then_inc(cut_f32_ok, 1)
            dve.wait_ge(cut_f32_ok, 2 * len(per_k))
            dve.wait_ge(rank_in, 16)
            for k, fs in per_k.items():
                row, lo = rank[:, 0:k], cut[k][3]
                rows = bass.AP(tensor=row.tensor, offset=row.offset, ap=[list(row.ap[0]), [0, len(fs)], list(row.ap[1])])
                los = bass.AP(tensor=lo.tensor, offset=lo.offset, ap=[list(lo.ap[0]), list(lo.ap[1]), [0, k]])
                at = mask_at[fs[0]]
                nc.vector.tensor_tensor(mask[:, at:at + len(fs) * k].rearrange("p (f k) -> p f k", k=k), rows, los,
                                        ALU.is_equal).then_inc(mask_ok, 1)

            def make_one_hot(b):
                k, _, fs = batches[b]
                dve.wait_ge(spread, b + 1)
                if b >= 2:
                    dve.wait_ge(looked_up, b - 1)
                w, parts = len(fs) * P, small_d[k].shape[0]
                nc.vector.tensor_scalar(one_hots[b % 2][0:parts, 0:w], l2_ps[0:parts, b % 2, 0:w],
                                        rank[0:parts, widest:widest + 1], None, ALU.is_equal).then_inc(one_hot, 1)

            def pick(b):
                k, _, fs = batches[b]
                dve.wait_ge(looked_up, b + 1)
                if b >= 1:
                    dve.wait_ge(picked, b)
                w = len(fs) * k * D
                m = mask[:, mask_at[fs[0]]:mask_at[fs[0]] + len(fs) * k]
                wide = bass.AP(tensor=m.tensor, offset=m.offset, ap=[list(m.ap[0]), list(m.ap[1]), [0, D]])
                nc.vector.tensor_tensor(chosen[:, 0:w].rearrange("p (r d) -> p r d", d=D),
                                        l2_ps[:, 2 + b % 2, 0:w].rearrange("p (r d) -> p r d", d=D), wide,
                                        ALU.mult).then_inc(masked, 1)
                dve.wait_ge(masked, b + 1)
                n = small.index(fs[0])
                nc.vector.tensor_reduce(looked[:, n * D:(n + len(fs)) * D].rearrange("p (n d) -> p n d", d=D),
                                        chosen[:, 0:w].rearrange("p (n k d) -> p n d k", k=k, d=D),
                                        mybir.AxisListType.X, ALU.add).then_inc(picked, 1)

            dve.wait_ge(mask_ok, len(per_k))
            make_one_hot(0)
            make_one_hot(1)
            for b in range(len(batches)):
                pick(b)
                if b + 2 < len(batches):
                    make_one_hot(b + 2)
                if b == W0_AFTER:
                    dve.wait_ge(w0_in, 32)
                    nc.vector.tensor_tensor(w0_s, w0_a, w0_b, ALU.add).then_inc(w0_sum, 1)

            def form_pairs(n, t, G, to):
                dve.wait_ge(shifted_in[t], 16 * (ROWS[t] // F) * G + 16 * (KPT if t < DIRECT else 1))
                r = ROWS[t]
                nc.vector.tensor_tensor(to[0:r, :], turn_ps[0:r, :], shifted[0:r, t, :],
                                        ALU.mult).then_inc(pairs_ok, 1)

            def keep_pair_lo(n, t, slot, bank):
                dve.wait_ge(pair_hi, n + 1 - KT)
                r = ROWS[t]
                nc.vector.tensor_tensor(pl[0:r, slot, :], bank[0:r, :], ph[0:r, slot, :].bitcast(F32),
                                        ALU.subtract).then_inc(pair_lo, 1)

            def keep_x1_lo(G, gi):
                dve.wait_ge(x1_hi, G + 1)
                nc.vector.tensor_tensor(x1l[:, gi % 2, :], l1_ps[:], x1h[:, gi % 2, :].bitcast(F32),
                                        ALU.subtract).then_inc(x1_lo, 1)

            def add_z1(G, gi):
                if gi == 0:
                    nc.vector.tensor_copy(z1acc[:], l1_ps[:]).then_inc(z1_added, 1)
                else:
                    dve.wait_ge(z1_added, G)
                    nc.vector.tensor_tensor(z1acc[:], l1_ps[:], z1acc[:], ALU.add).then_inc(z1_added, 1)

            def fma(G, gi, s, i, tt):
                p, j = s // 5, 2 * (s % 5)
                tile, f = 2 * p + tt, FOFF[j] + i
                if i == 0:
                    dve.wait_ge(y_ready, UNITS * G + 4 * s + tt + 1)
                e_col = e_cur[:, f, TPG * gi + tile:TPG * gi + tile + 1]
                y = l2_ps[:, tt, i * M:(i + 1) * M]
                acc = xd[:, gi % 2, tile, :]
                if f == 0:
                    nc.vector.tensor_scalar(acc, y, e_col, None, ALU.mult).then_inc(fma_done, 1)
                else:
                    before = fma_count(s, i - 1, tt) if i else fma_count(s - 1, NF[j - 2] - 1, tt)
                    dve.wait_ge(fma_done, FMAS * G + before)
                    nc.vector.scalar_tensor_tensor(out=acc, in0=y, scalar=e_col, in1=acc, op0=ALU.mult,
                                                   op1=ALU.add).then_inc(fma_done, 1)

            def join_last(p):
                n = CHUNKS * GROUPS - 1
                dve.wait_ge(fma_done, FMAS * n + FMAS // 2 * (p + 1))
                dve.wait_ge(pool_added, ADDS * n + (ADDS // 2 if p == 0 else ADDS - 3))
                nc.vector.tensor_tensor(xd[:, 1, 2 * p:2 * p + 2], xd[:, 1, 2 * p:2 * p + 2],
                                        xp[:, 1, 2 * p:2 * p + 2], ALU.add).then_inc(x2_ready, 1)

            def join_x2(G, par):
                dve.wait_ge(fma_done, FMAS * (G + 1))
                dve.wait_ge(pool_added, ADDS * (G + 1))
                nc.vector.tensor_tensor(xd[:, par], xd[:, par], xp[:, par], ALU.add).then_inc(x2_ready, 1)

            def fold_z1(c, first):
                dve.wait_ge(z1_added, GROUPS * (c + 1))
                if not first:
                    dve.wait_ge(h1_done, c)
                nc.vector.tensor_tensor(z1acc[:, 0:2 * P], z1acc[:, 0:2 * P], z1acc[:, 2 * P:4 * P],
                                        ALU.add).then_inc(z1_fold, 1)
                dve.wait_ge(z1_fold, 2 * c + 1)
                nc.vector.tensor_tensor(z1t[:], z1acc[:, 0:P], z1acc[:, P:2 * P], ALU.add).then_inc(z1_fold, 1)
                dve.wait_ge(z1_fold, 2 * c + 2)

            def relu_h1(c, bank):
                dve.wait_ge(h1_done, c + 1)
                nc.vector.tensor_scalar(h1s[:], bank[:], 0.0, None, ALU.max).then_inc(h1_ready, 1)

            def relu_h2(c):
                dve.wait_ge(h2_done, c + 1)
                nc.vector.tensor_scalar(h2s[:], l3_ps[:, 0:H2], 0.0, None, ALU.max).then_inc(h2_ready, 1)

            def keep_y(c):
                dve.wait_ge(y_done, c + 1)
                nc.vector.tensor_scalar(y_sb[:, bass.ds(c * P, P)], l3_ps[0:1, 0:P], 1.0, None,
                                        ALU.mult).then_inc(y_kept, 1)

            def keep_e(c):
                dve.wait_ge(gathered, gathers(c))
                if isinstance(c, int) and c == 0:
                    dve.wait_ge(looked_kept, len(small))
                nc.vector.tensor_copy(e_cur[:], e_next[:]).then_inc(e_cur_ok, 1)
                dve.wait_ge(e_cur_ok, c + 1)

            keep_e(0)
            dve.wait_ge(w0h_ok, 1)
            nc.vector.tensor_tensor(w0l[0:ROWS[0], :], w0_s, w0h[0:ROWS[0], :].bitcast(F32),
                                    ALU.subtract).then_inc(w0l_ok, 1)
            dve.wait_ge(w1h_ok, 1)
            nc.vector.tensor_tensor(w1l[:, 0:W1_CUT], w1_raw[:, 0:W1_CUT], w1h[:, 0:W1_CUT].bitcast(F32),
                                    ALU.subtract).then_inc(w1l_ok, 1)
            dve.wait_ge(turned_ps, 1)
            for t in range(KT):
                form_pairs(t, t, 0, shifted[:, t, :])
            keep_x1_lo(0, 0)
            add_z1(0, 0)

            def chunk(c, first, last):
                if not first:
                    dve.wait_ge(fma_done, FMAS * GROUPS * c)
                    keep_e(c)
                for gi in range(GROUPS):
                    G = 4 * c + gi
                    ahead = not (last and gi == GROUPS - 1)
                    if not (first and gi < 2):
                        dve.wait_ge(x2_stored, 16 * (G - 1))
                    for s in range(SLOTS):
                        for i, tt in fma_order(s):
                            fma(G, gi, s, i, tt)
                        if ahead and 1 <= s <= KT:
                            keep_pair_lo(KT * (G + 1) + s - 1, s - 1, (KT * (gi + 1) + s - 1) % 2, pair_ps)
                        if ahead and s < KT:
                            if not (first and gi == 0 and s == 0):
                                dve.wait_ge(pair_lo, KT * G + s)
                            form_pairs(KT * (G + 1) + s, s, G + 1, pair_ps)
                        if ahead and s == KT + 1:
                            keep_x1_lo(G + 1, (gi + 1) % GROUPS)
                        if ahead and s == KT + 2:
                            add_z1(G + 1, (gi + 1) % GROUPS)
                        if s == 3 and not (first and gi == 0):
                            join_x2(G - 1, (gi - 1) % 2)
                        if last and gi == GROUPS - 1 and s == SLOTS - 1:
                            join_last(0)
                        if gi == 3 and s == 5:
                            if not first:
                                relu_h1(c - 1, l3_ps)
                            fold_z1(c, first)
                        if gi == 3 and s == 8 and not first:
                            relu_h2(c - 1)
                if not first:
                    keep_y(c - 1)

            chunk(0, True, False)
            with dve.Fori(1, CHUNKS - 1) as c:
                chunk(c, False, False)
            chunk(CHUNKS - 1, False, True)
            end = CHUNKS - 1
            n = CHUNKS * GROUPS - 1
            dve.wait_ge(act_scaled, SCALED * CHUNKS * GROUPS)
            dve.wait_ge(pool_added, ADDS * n + ADDS - 6)
            s3, s4 = scaled[:, 7, :], scaled[:, 9, :]
            nc.vector.tensor_tensor(s3, s3, s4, ALU.add).then_inc(last_added, 1)
            dve.wait_ge(last_added, 1)
            nc.vector.tensor_tensor(s3[:, 0:2 * M], s3[:, 0:2 * M], s3[:, 2 * M:4 * M], ALU.add).then_inc(last_added, 1)
            dve.wait_ge(last_added, 2)
            nc.vector.tensor_tensor(xp[:, 1, 3, :], s3[:, 0:M], s3[:, M:2 * M], ALU.add).then_inc(last_added, 1)
            dve.wait_ge(last_added, 3)
            join_last(1)
            relu_h1(end, l1_ps)
            relu_h2(end)
            keep_y(end)

        @block.tensor
        def _(pe):
            def turn(G):
                pe.wait_ge(tripled_ok, G + 1)
                if not (isinstance(G, int) and G == 0):
                    pe.wait_ge(pairs_ok, KT * G)
                for k in range(TPG):
                    last = nc.tensor.transpose(turn_ps[0:KPT * F, k * P:(k + 1) * P],
                                               tripled[:, k].rearrange("p k f -> p (k f)"), ident[:])
                last.then_inc(turned_ps, 1)

            def contract_pairs(n, t, slot):
                pe.wait_ge(pair_lo, n + 1 - KT)
                r = ROWS[t]
                w = slice(t * M, (t + 1) * M)
                nc.tensor.matmul(l1_ps[:], w0h[0:r, w], ph[0:r, slot, :], start=(t == 0), stop=False)
                nc.tensor.matmul(l1_ps[:], w0h[0:r, w], pl[0:r, slot, :], start=False, stop=False)
                nc.tensor.matmul(l1_ps[:], w0l[0:r, w], ph[0:r, slot, :], start=False,
                                 stop=(t == KT - 1)).then_inc(l1_done, 1)

            def layer2(G, gi, u, first):
                p, j, tt = u // 20, (u % 20) // 2, u % 2
                if not (first and gi == 0 and u < 4):
                    if j % 2 == 0:
                        before = u // 4 - 1 if u >= 4 else SLOTS - 1
                        pe.wait_ge(fma_done, FMAS * (G if u >= 4 else G - 1) +
                                   fma_count(before, NF[2 * (before % 5)] - 1, tt))
                    else:
                        pe.wait_ge(act_scaled, SCALED * G + 10 * p + j - 2 + tt)
                cols = slice((2 * p + tt) * P, (2 * p + tt + 1) * P)
                rows = slice(FOFF[j] * M, (FOFF[j] + NF[j]) * M)
                y = l2_ps[:, u % 4, 0:NF[j] * M]
                xh, xl = x1h[:, gi % 2, cols], x1l[:, gi % 2, cols]
                nc.tensor.matmul(y, xh, w1h[:, rows], start=True, stop=False)
                nc.tensor.matmul(y, xh, w1l[:, rows], start=False, stop=False)
                nc.tensor.matmul(y, xl, w1h[:, rows], start=False, stop=True).then_inc(y_ready, 1)

            def layer3_g(c, q, bank, free=True):
                if q == 0:
                    pe.wait_ge(x2q_in, 16 * D * (c + 1))
                    pe.wait_ge(eblk_in, 16 * SB8 * (c + 1))
                elif free:
                    pe.wait_ge(g_kept, QS * c + q)
                nc.tensor.matmul(bank[:, 0:SB8 * FG], x2q[:, q, :], eblk[:, q, :], start=True,
                                 stop=True).then_inc(g_done, 1)

            def layer3_f(c, f):
                if f == 0:
                    pe.wait_ge(g_kept, QS * (c + 1))
                mm = nc.tensor.matmul(l3_ps[:, 0:P], w2[:, f, :], gs[:, f, :], start=(f == 0), stop=(f == F - 1))
                if f == F - 1:
                    mm.then_inc(z3_done, 1)

            def mlp1_early(c, m, bank, start=True):
                if m == 0:
                    pe.wait_ge(z1_fold, 2 * (c + 1))
                cols = slice(m * P, (m + 1) * P)
                nc.tensor.matmul(bank[:, cols], wt1[:, 0, cols], z1t[:], start=start, stop=False)
                nc.tensor.matmul(bank[:, cols], wtd[:, cols], dense_sb[:, bass.ds(c * P, P)], start=False, stop=False)

            def mlp1_late(c, m, bank, stop=True):
                if m == 0:
                    pe.wait_ge(z3_ready, c + 1)
                cols = slice(m * P, (m + 1) * P)
                nc.tensor.matmul(bank[:, cols], wt1[:, 1, cols], gs[:, F, :], start=False, stop=False)
                mm = nc.tensor.matmul(bank[:, cols], wt1[:, 2, cols], z3t[:], start=False, stop=stop)
                if m == H1 // P - 1:
                    mm.then_inc(h1_done, 1)

            def mlp2(c, m):
                if m == 0:
                    pe.wait_ge(h1_ready, c + 1)
                cols = slice(m * P, (m + 1) * P)
                for k in range(H1 // P):
                    nc.tensor.matmul(l3_ps[:, cols], wt2[:, k, cols], h1s[:, k * P:(k + 1) * P],
                                     start=(k == 0), stop=False)
                mm = nc.tensor.matmul(l3_ps[:, cols], bt2[:, cols], ones_row[:], start=False, stop=True)
                if m == H2 // P - 1:
                    mm.then_inc(h2_done, 1)

            def mlp3(c):
                pe.wait_ge(h2_ready, c + 1)
                for k in range(H2 // P):
                    mm = nc.tensor.matmul(l3_ps[0:1, 0:P], wt3[:, k:k + 1], h2s[:, k * P:(k + 1) * P],
                                          start=(k == 0), stop=(k == H2 // P - 1))
                mm.then_inc(y_done, 1)

            def spread_indices(b):
                k, first_f, fs = batches[b]
                parts = small_d[k].shape[0]
                for i in range(len(fs)):
                    n = first_f + i
                    col = cut[k][2][:, n:n + 1]
                    rep = bass.AP(tensor=col.tensor, offset=col.offset, ap=[list(col.ap[0]), [0, parts]])
                    mm = nc.tensor.matmul(l2_ps[0:parts, b % 2, i * P:(i + 1) * P], rep, ident[:],
                                          start=True, stop=True)
                mm.then_inc(spread, 1)

            pe.wait_ge(ident_ok, 1)
            pe.wait_ge(cut_f32_ok, 2 * len(per_k))
            spread_indices(0)
            spread_indices(1)
            pe.wait_ge(tables_in, 16 * len(per_k))
            for b, (k, first_f, fs) in enumerate(batches):
                pe.wait_ge(one_hot, b + 1)
                if b >= 2:
                    pe.wait_ge(masked, b - 1)
                parts = small_d[k].shape[0]
                for i in range(len(fs)):
                    n = first_f + i
                    mm = nc.tensor.matmul(l2_ps[:, 2 + b % 2, i * k * D:(i + 1) * k * D],
                                          one_hots[b % 2][0:parts, i * P:(i + 1) * P],
                                          small_tables[k][:, n * k * D:(n + 1) * k * D], start=True, stop=True)
                mm.then_inc(looked_up, 1)
                if b + 2 < len(batches):
                    spread_indices(b + 2)

            turn(0)
            pe.wait_ge(w0_sum, 1)
            for t in range(KT):
                pe.wait_ge(pairs_ok, t + 1)
                nc.tensor.matmul(l1_ps[:], w0_s[0:ROWS[t], t * M:(t + 1) * M], shifted[0:ROWS[t], t, :],
                                 start=(t == 0), stop=(t == KT - 1)).then_inc(l1_done, 1)
            turn(1)
            pe.wait_ge(w1l_ok, 2)
            pe.wait_ge(w0l_ok, 1)

            def layer3_and_mlp(c, gi, s, v):
                q = 2 * (SLOTS * gi + s - G_SLOT) + v // 2
                if v % 2 and 0 <= q < QS:
                    layer3_g(c, q, l3_ps)
                f = 3 * (SLOTS * gi + s - F_SLOT) + (0, 1, 0, 2)[v]
                if v != 2 and 0 <= f < F:
                    layer3_f(c, f)
                if gi == 3 and v == 3 and s < H1 // P:
                    if s == 0:
                        pe.wait_ge(z3_ready, c + 1)
                    mlp1_early(c, s, l3_ps)
                    mlp1_late(c, s, l3_ps)
                if gi == 3 and v == 3 and 6 <= s < 6 + H2 // P:
                    mlp2(c, s - 6)

            def chunk(c, first, last):
                for gi in range(GROUPS):
                    G = 4 * c + gi
                    ahead = not (last and gi == GROUPS - 1)
                    pe.wait_ge(x1_lo, G + 1)
                    for s in range(SLOTS):
                        for v in range(4):
                            layer2(G, gi, 4 * s + v, first)
                            if v == 1 and ahead and 2 <= s < 2 + KT:
                                t = s - 2
                                if t == 0:
                                    pe.wait_ge(z1_added, G + 1)
                                contract_pairs(KT * (G + 1) + t, t, (KT * (gi + 1) + t) % 2)
                            if not first:
                                layer3_and_mlp(c - 1, gi, s, v)
                        if s == TURN_SLOT and not (last and gi >= GROUPS - 2):
                            turn(G + 2)
                if not first:
                    mlp3(c - 1)

            chunk(0, True, False)
            pe.wait_ge(w2_in, 16)
            pe.wait_ge(top_in, 96)
            pe.wait_ge(filled, 3)
            pe.wait_ge(dense_in, 16)
            with pe.Fori(1, CHUNKS - 1) as c:
                chunk(c, False, False)
            chunk(CHUNKS - 1, False, True)
            end = CHUNKS - 1
            pe.wait_ge(z1_added, CHUNKS * GROUPS)
            for m in range(H1 // P):
                mlp1_early(end, m, l1_ps, m == 0)
            for q in range(QS):
                if q >= 4:
                    pe.wait_ge(g_kept, QS * end + q - 3)
                layer3_g(end, q, l2_ps[:, q % 4, :], False)
            for f in range(F):
                layer3_f(end, f)
            for m in range(H1 // P):
                mlp1_late(end, m, l1_ps, m == H1 // P - 1)
            for m in range(H2 // P):
                mlp2(end, m)
            mlp3(end)


def kernel(**inputs):
    import concourse.bacc as _bacc
    from concourse.bass_utils import run_bass_kernel_spmd as _run

    f0 = np.asarray(inputs["L0_rec_f0"])
    a, b = pair_rows()
    w0 = np.zeros((2, KT * KPT * F, M), f0.dtype)
    w0[0, :a.size] = f0[a]
    w0[1, F:b.size] = f0[b[F:]]
    w0 = np.ascontiguousarray(w0.reshape(2, KT, KPT * F, M).transpose(0, 2, 1, 3)).reshape(2, KPT * F, KT * M)
    arrays = {"ids": np.ascontiguousarray(inputs["ids"])}
    for f in range(F):
        arrays[f"tbl_{f}"] = np.ascontiguousarray(inputs[f"tbl_{f}"])
    arrays["w0a"], arrays["w0b"] = np.ascontiguousarray(w0[0]), np.ascontiguousarray(w0[1])
    for name, key in (("f1", "L0_rec_f1"), ("f2", "L0_rec_f2"), ("wt1", "W_top1"), ("wt2", "W_top2")):
        arrays[name] = np.ascontiguousarray(inputs[key])
    arrays["wt3"] = np.ascontiguousarray(np.asarray(inputs["W_top3"]).reshape(H2 // P, P).T)
    arrays["bt1"] = np.ascontiguousarray(inputs["b_top1"]).reshape(1, H1)
    arrays["bt2"] = np.ascontiguousarray(inputs["b_top2"]).reshape(1, H2)
    arrays["dense_t"] = np.ascontiguousarray(np.asarray(inputs["dense_ctx"]).T)

    widest = max(SMALL_K.values())
    arrays["rank"] = np.concatenate([np.tile(np.arange(widest), (P, 1)), np.arange(P)[:, None]], axis=1,
                                    dtype=np.float32)
    per_k, _ = lookup_plan([arrays[f"tbl_{f}"].shape[0] for f in range(F)])
    for k, fs in per_k.items():
        parts = -(-arrays[f"tbl_{fs[0]}"].shape[0] // k)
        small = np.zeros((parts * k, len(fs), D), arrays[f"tbl_{fs[0]}"].dtype)
        for i, f in enumerate(fs):
            small[:arrays[f"tbl_{f}"].shape[0], i] = arrays[f"tbl_{f}"]
        arrays[f"small_ids{k}"] = np.ascontiguousarray(arrays["ids"][0:P, fs])
        arrays[f"small{k}"] = np.ascontiguousarray(
            small.reshape(parts, k, len(fs), D).transpose(0, 2, 1, 3)).reshape(parts, len(fs) * k * D)

    nc = _bacc.Bacc("TRN2", target_bir_lowering=False, num_devices=1)
    ap = {k: nc.dram_tensor(f"in_{k}", v.shape, mybir.dt.from_np(v.dtype), kind="ExternalInput").ap()
          for k, v in arrays.items()}
    out = nc.dram_tensor("out_y", (1, B), F32, kind="ExternalOutput").ap()
    build(nc, ap["ids"], [ap[f"tbl_{f}"] for f in range(F)], ap["w0a"], ap["w0b"], ap["f1"], ap["f2"],
          ap["wt1"], ap["bt1"], ap["wt2"], ap["bt2"], ap["wt3"], ap["dense_t"], ap["rank"],
          {k: ap[f"small{k}"] for k in per_k}, {k: ap[f"small_ids{k}"] for k in per_k}, out)
    r = _run(nc, [{f"in_{k}": v for k, v in arrays.items()}], core_ids=[0])
    return r.results[0]["out_y"].reshape(B, 1)
```
